# Optimizing a Trainium2 kernel written in Bass

```python
import numpy as np
import jax
import jax.numpy as jnp

def _softmax(x, axis=-1):
    return jax.nn.softmax(x, axis=axis)

def _gelu(x):
    return jax.nn.gelu(x, approximate=True)

def _silu(x):
    return jax.nn.silu(x)

def _sigmoid(x):
    return jax.nn.sigmoid(x)

def _layernorm(x, axis=-1, eps=1e-05):
    m = jnp.mean(x, axis=axis, keepdims=True)
    v = jnp.var(x, axis=axis, keepdims=True)
    return (x - m) / jnp.sqrt(v + eps)

def _scatter_add(tgt, idx, src, axis=0):
    return tgt.at[idx].add(src)

def _segment_sum(src, seg, n):
    return jax.ops.segment_sum(src, seg, n)
kernel_name = 'mk_gnn_resnorm_d2_gnn_r32_fd75a5'

def setup_inputs(seed: int=0):
    np.random.seed(seed)
    _w = jnp.asarray

    def _rec_inputs():
        import jax
        import jax.numpy as jnp
        _gk = jax.random.key(seed)
        x = -0.0003713 + 1 * jax.random.normal(jax.random.fold_in(_gk, 1), (3125, 256), jnp.float32)
        _s = jax.random.randint(jax.random.fold_in(_gk, 2), (25000,), 0, 3125, jnp.int32)
        _d = jax.random.randint(jax.random.fold_in(_gk, 3), (25000,), 0, 3125, jnp.int32)
        _loop = jnp.arange(3125, dtype=jnp.int32)
        src = jnp.concatenate([_s, _d, _loop])
        dst = jnp.concatenate([_d, _s, _loop])
        _o = jnp.argsort(dst, stable=True)
        src = src[_o]
        dst = dst[_o]
        edge_type_200 = jax.random.randint(jax.random.fold_in(_gk, 12), (53125,), 0, 200, jnp.int32)
        return (x, src, dst, edge_type_200)
    x, src, dst, edge_type_200 = _rec_inputs()

    def _L0_gnn_setup():
        import jax, jax.numpy as jnp
        import numpy as np
        N, D, E, R = (50000, 256, 20000, 200)
        if __name__ == '__main__':
            out = reference(**setup_inputs())
            print(out.shape, out.dtype)
        key = jax.random.key(seed)
        ks = jax.random.split(key, 12)

        def xavier(k, shape, gain=np.sqrt(2.0)):
            fan_in, fan_out = (shape[0], shape[1])
            bound = gain * np.sqrt(6.0 / (fan_in + fan_out))
            return jax.random.uniform(k, shape, jnp.float32, -bound, bound)
        return {'h': jax.random.normal(ks[0], (N, D), jnp.float32), 'rel_emb': jax.random.normal(ks[1], (R, D), jnp.float32) * 0.1, 'weight_neighbor': xavier(ks[2], (D, D)), 'a': xavier(ks[3], (3 * D, 1)), 'W3': xavier(ks[4], (3 * D, 3 * D)), 'loop_weight': xavier(ks[5], (D, D)), 'evolve_loop_weight': xavier(ks[6], (D, D)), 'src': jax.random.randint(ks[7], (E,), 0, N, jnp.int32), 'dst': jax.random.randint(ks[8], (E,), 0, N, jnp.int32), 'etype': jax.random.randint(ks[9], (E,), 0, R, jnp.int32)}
    _L0_gnn_all = _L0_gnn_setup()
    _L0_gnn_in = {k: v for k, v in _L0_gnn_all.items() if k in ('rel_emb', 'weight_neighbor', 'a', 'W3', 'loop_weight', 'evolve_loop_weight')}
    del _L0_gnn_all

    def _L1_gnn_setup():
        import jax, jax.numpy as jnp
        import numpy as np
        N = 3125
        E = 50000
        IN_FEATS = 256
        OUT_FEATS = 256
        MAXK = 32

        def _maxk(x, k):
            _, idx = jax.lax.top_k(x, k)
            rows = jnp.arange(x.shape[0])[:, None]
            mask = jnp.zeros_like(x).at[rows, idx].set(1.0)
            return x * mask
        key = jax.random.key(seed)
        k1, k2, k3, k4, k5 = jax.random.split(key, 5)
        feat = jax.random.normal(k1, (N, IN_FEATS), dtype=jnp.float32)
        W_self = jax.random.normal(k2, (IN_FEATS, OUT_FEATS), dtype=jnp.float32) * (1.0 / np.sqrt(IN_FEATS))
        W_neigh = jax.random.normal(k3, (IN_FEATS, OUT_FEATS), dtype=jnp.float32) * (1.0 / np.sqrt(IN_FEATS))
        src = jax.random.randint(k4, (E,), 0, N, dtype=jnp.int64)
        dst = jax.random.randint(k5, (E,), 0, N, dtype=jnp.int64)
        return {'feat': feat, 'W_self': W_self, 'W_neigh': W_neigh, 'src': src, 'dst': dst}
    _L1_gnn_all = _L1_gnn_setup()
    _L1_gnn_in = {k: v for k, v in _L1_gnn_all.items() if k in ('W_self', 'W_neigh')}
    del _L1_gnn_all
    return {'x': x, 'src': src, 'dst': dst, 'edge_type_200': edge_type_200, 'L0_gnn_rel_emb': _L0_gnn_in['rel_emb'], 'L0_gnn_weight_neighbor': _L0_gnn_in['weight_neighbor'], 'L0_gnn_a': _L0_gnn_in['a'], 'L0_gnn_W3': _L0_gnn_in['W3'], 'L0_gnn_loop_weight': _L0_gnn_in['loop_weight'], 'L0_gnn_evolve_loop_weight': _L0_gnn_in['evolve_loop_weight'], 'L1_gnn_W_self': _L1_gnn_in['W_self'], 'L1_gnn_W_neigh': _L1_gnn_in['W_neigh']}

def reference(x, src, dst, edge_type_200, L0_gnn_rel_emb, L0_gnn_weight_neighbor, L0_gnn_a, L0_gnn_W3, L0_gnn_loop_weight, L0_gnn_evolve_loop_weight, L1_gnn_W_self, L1_gnn_W_neigh):
    import jax
    import jax.numpy as jnp

    def _L0_gnn_ref(h, rel_emb, weight_neighbor, a, W3, loop_weight, evolve_loop_weight, src, dst, etype):
        import jax, jax.numpy as jnp
        import numpy as np
        N, D, E, R = (50000, 256, 20000, 200)
        if __name__ == '__main__':
            out = reference(**setup_inputs())
            print(out.shape, out.dtype)
        n, d = h.shape
        e = src.shape[0]
        in_deg = jax.ops.segment_sum(jnp.ones((e,), h.dtype), dst, num_segments=n)
        loop_message = jnp.where((in_deg > 0)[:, None], h @ loop_weight, h @ evolve_loop_weight)
        W = (W3 @ a)[:, 0]
        w_src, w_dst, w_rel = (W[:d], W[d:2 * d], W[2 * d:])
        rel_e = rel_emb[etype]
        score = h[src] @ w_src + h[dst] @ w_dst + rel_e @ w_rel
        alpha = jnp.exp(jax.nn.leaky_relu(score))[:, None]
        alpha = alpha / jnp.sum(alpha, axis=1, keepdims=True)
        msg = (h[src] + rel_e) @ weight_neighbor * alpha
        agg = jax.ops.segment_sum(msg, dst, num_segments=n)
        node_repr = jax.nn.relu(agg) + loop_message
        return node_repr

    def _L1_gnn_ref(feat, W_self, W_neigh, src, dst):
        import jax, jax.numpy as jnp
        import numpy as np
        N = 3125
        E = 50000
        IN_FEATS = 256
        OUT_FEATS = 256
        MAXK = 32

        def _maxk(x, k):
            _, idx = jax.lax.top_k(x, k)
            rows = jnp.arange(x.shape[0])[:, None]
            mask = jnp.zeros_like(x).at[rows, idx].set(1.0)
            return x * mask
        n = feat.shape[0]
        h_self = feat @ W_self
        h_neigh = feat @ W_neigh
        h_sparse = _maxk(h_neigh, MAXK)
        msg = h_sparse[src]
        summed = jax.ops.segment_sum(msg, dst, num_segments=n)
        deg = jax.ops.segment_sum(jnp.ones((src.shape[0],), dtype=feat.dtype), dst, num_segments=n)
        neigh = summed / jnp.maximum(deg, 1.0)[:, None]
        return h_self + neigh
    x = _layernorm(x + _L0_gnn_ref(x, L0_gnn_rel_emb, L0_gnn_weight_neighbor, L0_gnn_a, L0_gnn_W3, L0_gnn_loop_weight, L0_gnn_evolve_loop_weight, src, dst, edge_type_200), axis=-1)
    x = _layernorm(x + _L1_gnn_ref(x, L1_gnn_W_self, L1_gnn_W_neigh, src, dst), axis=-1)
    return x

_drawn_inputs = setup_inputs


def setup_inputs(seed=0):
    import zlib

    import numpy as np

    out = dict(_drawn_inputs(seed))
    spreads = {}
    factors = {}
    for name, (base, spread) in spreads.items():
        noise = np.random.default_rng([zlib.crc32(name.encode()), seed]).standard_normal(out[name].shape)
        drawn = base * np.exp(spread * noise) if base else spread * noise
        out[name] = jnp.asarray(drawn.astype(out[name].dtype))
    for name, factor in factors.items():
        out[name] = (out[name] * factor).astype(out[name].dtype)
    return out
```

```python
from contextlib import ExitStack

import concourse.bass as bass
from concourse import mybir



def gnn_two_layers(nc, x, src, dst, etype, rel_emb, w_neighbor, a, w3, loop_w, evolve_w, w_self, w_neigh, out):
    f32, i32, bf16 = mybir.dt.float32, mybir.dt.int32, mybir.dt.bfloat16
    ALU, ACT, AX = mybir.AluOpType, mybir.ActivationFunctionType, mybir.AxisListType
    RMAX = bass.bass_isa.ReduceOp.max

    P = 128
    N, D = x.shape
    E = src.shape[0]
    R = rel_emb.shape[0]
    KD = D // P
    NT = -(-N // P)
    TAIL = N - (NT - 1) * P
    NPAD = NT * P
    EFULL = E // P
    EREM = E - EFULL * P
    GT = 8
    SLOTS = 4
    NG = -(-(EFULL + 1) // (GT * SLOTS)) * SLOTS
    ITERS = NG // SLOTS
    NE = NG * GT
    LOOK = 2
    RC = 4
    RP = NE // RC
    STAGES = NG + LOOK
    ROW0 = 272
    NACC = N + P
    TOPK = 32
    EPS = 1e-5
    LOWEST = -3.4028234663852886e38
    MAXPASS = NT

    table0 = nc.dram_tensor("table0", (NPAD, ROW0), f32).ap()
    table1 = nc.dram_tensor("table1", (NPAD, D), f32).ap()

    ctx = ExitStack()
    with ctx:
        def sb(name, shape, dt=f32):
            return ctx.enter_context(nc.sbuf_tensor(name, shape, dt))

        def sem(name):
            return ctx.enter_context(nc.semaphore(name))

        ident = sb("ident", [P, P])
        iota = sb("iota", [P, 256])
        ones = sb("ones", [P, P])
        eps_t = sb("eps_t", [P, 1])
        x_sb = sb("x_sb", [P, NT, D])
        xT = sb("xT", [P, KD, NPAD])
        sums = sb("sums", [P, 4, NACC])
        dst_score = sb("dst_score", [P, NACC])
        rel_score = sb("rel_score", [P, R])
        rows = sb("rows", [P, SLOTS, GT, ROW0])
        hot_dst = sb("hot_dst", [P, 2, GT, P])
        hot_dst_b = sb("hot_dst_b", [P, 2, GT, P], bf16)
        hot_rel = sb("hot_rel", [P, 2, GT, 256], bf16)
        w_tab = sb("w_tab", [P, KD, D + 1])
        w_loops = sb("w_loops", [P, KD, 2 * D])
        w_l1 = sb("w_l1", [P, KD, 2 * D])
        w_vec = sb("w_vec", [P, 6])
        wd_bc = sb("wd_bc", [P, KD, P])
        rel_tab = sb("rel_tab", [P, 2, D + 1])
        tabs = sb("tabs", [P, 3, STAGES * GT])
        dst_f = sb("dst_f", [P, NE])
        idx_tab = sb("idx_tab", [P, STAGES * GT], i32)
        tab_slot = sb("tab_slot", [P, SLOTS, 3, GT])
        idx_slot = [sb(f"idx_slot{s}", [P, GT], i32) for s in range(SLOTS)]
        span_in = sb("span_in", [P, 2, NG])
        span = sb("span", [P, 2, NG])
        base0 = sb("base0", [P, NG])
        base_cur = sb("base_cur", [P, NG])
        base_i = sb("base_i", [P, 1 + NG], i32)
        flags = sb("flags", [P, 8])
        passes_i = sb("passes_i", [P, 1], i32)
        score_dst = sb("score_dst", [P, 2, GT])
        score_rel = sb("score_rel", [P, 2, GT])
        sc = sb("sc", [P, 2, 6, GT])
        r_deg = sb("r_deg", [P, NT])
        node_slots = sb("node_slots", [P, 4, D])
        xs = node_slots[:, 0:2, :]
        xTs = node_slots[:, 2:4, :].rearrange("p u (c n) -> p u c n", c=KD)
        products = node_slots[:].rearrange("p a f -> p (a f)")[:, 0:GT * R // 2].bitcast(bf16).rearrange(
            "p (k r) -> p k r", k=GT)
        tab_out = sb("tab_out", [P, 2, ROW0])
        col = sb("col", [P, 2, 8])
        bn = sb("bn", [P, 2, 6])
        mv = sb("mv", [P, 2, 2])
        a_bc = hot_dst[:, 0, :, :].rearrange("p k n -> p (k n)")[:, 0:3 * D]
        rows_flat = rows[:].rearrange("p s k w -> p (s k w)")
        flat_used = [0]

        def in_rows(*shape):
            n = 1
            for d in shape:
                n *= d
            at = flat_used[0]
            flat_used[0] += n
            assert flat_used[0] <= SLOTS * GT * ROW0
            names = "abcd"[:len(shape)]
            return rows_flat[:, at:at + n].rearrange(f"p ({' '.join(names)}) -> p {' '.join(names)}",
                                                     **dict(zip(names, shape)))

        w3_sb = in_rows(6, 3 * D)
        rel_sb = in_rows(2, D)
        relT = in_rows(KD, 256)
        wr_bc = in_rows(KD, P)
        iota_i = in_rows(256).bitcast(i32)
        edge_rows = in_rows(3, RC, P).bitcast(i32)[0:RP]
        flat_used[0] = 0
        x1Ts = in_rows(2, D)
        acc_s = in_rows(2, 4, P)
        yb = in_rows(2, 3, D)
        x1s = in_rows(2, D)
        hn = in_rows(2, D)
        work = in_rows(2, D)
        sparse = in_rows(2, D)
        edge_f = hot_rel[:].rearrange("p s k w -> p (s k w)").bitcast(f32)[0:RP, 0:3 * RC * P].rearrange(
            "p (a c i) -> p a c i", a=3, c=RC)
        top8 = sb("top8", [P, 2, 8])

        ps = [ctx.enter_context(nc.psum_tensor(f"ps{b}", [P, 512], f32)) for b in range(8)]

        s_ident = sem("s_ident")
        s_pads = sem("s_pads")
        s_ones = sem("s_ones")
        s_edges = sem("s_edges")
        s_rel = sem("s_rel")
        s_w3 = sem("s_w3")
        s_wn = sem("s_wn")
        s_x = sem("s_x")
        s_w = sem("s_w")
        s_w_plus = sem("s_w_plus")
        s_zero = sem("s_zero")
        s_edge_f = sem("s_edge_f")
        s_edge_t = sem("s_edge_t")
        s_span = sem("s_span")
        s_spanned = sem("s_spanned")
        s_passes = sem("s_passes")
        s_wvec = sem("s_wvec")
        s_relT = sem("s_relT")
        s_relT_sb = sem("s_relT_sb")
        s_relp = sem("s_relp")
        s_setup = sem("s_setup")
        s_xs = sem("s_xs")
        s_xt = sem("s_xt")
        s_xTs = sem("s_xTs")
        s_xT = sem("s_xT")
        s_tab_ps = sem("s_tab_ps")
        s_tab_sb = sem("s_tab_sb")
        s_t0 = [sem(f"s_t0_{u}") for u in range(2)]
        s_acc = sem("s_acc")
        s_agg = sem("s_agg")
        s_mask = sem("s_mask")
        s_loopm = sem("s_loopm")
        s_joined = sem("s_joined")
        s_var = sem("s_var")
        s_std = sem("s_std")
        s_rstd = sem("s_rstd")
        s_x1 = sem("s_x1")
        s_x1t = sem("s_x1t")
        s_x1T = sem("s_x1T")
        s_l1 = sem("s_l1")
        s_hn = sem("s_hn")
        s_res = sem("s_res")
        s_sparse = sem("s_sparse")
        s_t1 = [sem(f"s_t1_{u}") for u in range(2)]
        s_rezero = sem("s_rezero")
        s_facc = sem("s_facc")
        s_fagg = sem("s_fagg")
        s_fvar = sem("s_fvar")
        s_fstd = sem("s_fstd")
        s_frstd = sem("s_frstd")
        s_fout = sem("s_fout")
        s_out = [sem(f"s_out{u}") for u in range(2)]

        class Layer:
            def __init__(self, tag):
                self.base = sem(f"base_ready{tag}")
                self.staged = sem(f"staged{tag}")
                self.allowed = sem(f"allowed{tag}")
                self.gathered = [sem(f"gathered{tag}_{s}") for s in range(SLOTS)]
                self.hot_rel = sem(f"hot_rel{tag}")
                self.score = sem(f"score{tag}")
                self.alpha = sem(f"alpha{tag}")
                self.hot_dst = sem(f"hot_dst{tag}")
                self.hot_dst_b = sem(f"hot_dst_b{tag}")
                self.summed = sem(f"summed{tag}")
                self.added = sem(f"added{tag}")

        L0, L1 = Layer("0"), Layer("1")

        def over_tiles(eng, step):
            for T in range(4):
                step(T, T % 2, T // 2)
            with eng.Fori(0, (NT - 7) // 2) as it:
                step(it * 2 + 4, 0, it + 2)
                step(it * 2 + 5, 1, it + 2)
            for T in range(NT - 3, NT):
                step(T, T % 2, T // 2)

        def known(T, test):
            return isinstance(T, int) and test(T)

        def free_of(eng, done, T):
            if not known(T, lambda t: t < 2):
                eng.wait_ge(done, T - 1)

        def tile_cols(T):
            return bass.ds(T * P, P)

        block = ctx.enter_context(nc.Block())

        @block.sync
        def _(sp):
            sp.wait_ge(s_pads, 5)
            for k, e in enumerate((dst, src, etype)):
                whole = (RC - 1) * RP * P
                sp.dma_start(edge_rows[:, k, 0:RC - 1, :],
                             e[0:whole].rearrange("(c r i) -> r c i", c=RC - 1, i=P)).then_inc(s_edges, 16)
                more = EFULL - (RC - 1) * RP
                sp.dma_start(edge_rows[0:more, k, RC - 1, :],
                             e[whole:EFULL * P].rearrange("(r i) -> r i", i=P)).then_inc(s_edges, 16)
                sp.dma_start(edge_rows[more:more + 1, k, RC - 1, 0:EREM],
                             e[EFULL * P:E].rearrange("(r i) -> r i", r=1)).then_inc(s_edges, 16)
            sp.dma_start(w3_sb, w3.rearrange("(c p) k -> p c k", p=P)).then_inc(s_w3, 16)
            sp.dma_start(a_bc, a.rearrange("k o -> o k").broadcast_to([P, 3 * D])).then_inc(s_w3, 16)
            sp.dma_start(rel_sb[:, 0, :], rel_emb[0:P, :]).then_inc(s_rel, 16)
            sp.dma_start(rel_sb[0:R - P, 1, :], rel_emb[P:R, :]).then_inc(s_rel, 16)
            sp.dma_start(w_tab[:, :, 0:D], w_neighbor.rearrange("(c p) f -> p c f", p=P)).then_inc(s_wn, 16)
            sp.dma_start(x_sb[:, 0:NT - 1, :], x[0:(NT - 1) * P, :].rearrange("(t p) f -> p t f", p=P)).then_inc(s_x, 16)
            sp.dma_start(x_sb[0:TAIL, NT - 1, :], x[(NT - 1) * P:N, :]).then_inc(s_x, 16)
            sp.dma_start(w_loops[:, :, 0:D], loop_w.rearrange("(c p) f -> p c f", p=P)).then_inc(s_w, 16)
            sp.dma_start(w_loops[:, :, D:2 * D], evolve_w.rearrange("(c p) f -> p c f", p=P)).then_inc(s_w, 16)
            sp.dma_start(w_l1[:, :, 0:D], w_self.rearrange("(c p) f -> p c f", p=P)).then_inc(s_w, 16)
            sp.dma_start(w_l1[:, :, D:2 * D], w_neigh.rearrange("(c p) f -> p c f", p=P)).then_inc(s_w, 16)

            def store_table0(T, u, before):
                sp.wait_ge(s_tab_sb, T + 1)
                sp.dma_start(table0[tile_cols(T), :], tab_out[:, u, :]).then_inc(s_t0[u], 16)
            over_tiles(sp, store_table0)

            def store_table1(T, u, before):
                sp.wait_ge(s_sparse, T + 1)
                sp.dma_start(table1[tile_cols(T), :], sparse[:, u, :]).then_inc(s_t1[u], 16)
            over_tiles(sp, store_table1)

            def store_out(T, u, before):
                sp.wait_ge(s_fout, T + 1)
                if known(T, lambda t: t == NT - 1):
                    sp.dma_start(out[(NT - 1) * P:N, :], x1s[0:TAIL, u, :]).then_inc(s_out[u], 16)
                else:
                    sp.dma_start(out[tile_cols(T), :], x1s[:, u, :]).then_inc(s_out[u], 16)
            over_tiles(sp, store_out)
            sp.wait_ge(s_out[0], 16 * ((NT + 1) // 2))
            sp.wait_ge(s_out[1], 16 * (NT // 2))

        @block.gpsimd
        def _(pool):
            for k, pad in enumerate((N, 0, 0)):
                pool.memset(edge_rows[:, k, RC - 1, :], pad).then_inc(s_pads, 1)
            pool.memset(rel_sb, 0.0).then_inc(s_pads, 1)
            pool.memset(x_sb[:, NT - 1, :], 0.0).then_inc(s_pads, 1)
            pool.memset(ident[:], 0.0).then_inc(s_ident, 1)
            pool.iota(iota_i, pattern=[[1, 256]], base=0, channel_multiplier=0).then_inc(s_ones, 1)
            pool.wait_ge(s_ident, 1)
            pool.affine_select(out=ident[:], in_=ident[:], compare_op=ALU.not_equal, fill=1.0, base=0,
                               pattern=[[-1, P]], channel_multiplier=1).then_inc(s_ident, 1)
            pool.memset(dst_score[:, NPAD:NACC], 0.0).then_inc(s_zero, 1)
            pool.wait_ge(s_span, 1)
            pool.partition_all_reduce(span[:].rearrange("p a g -> p (a g)"),
                                      span_in[:].rearrange("p a g -> p (a g)"), P, RMAX).then_inc(s_spanned, 1)
            pool.memset(sums[:], 0.0).then_inc(s_zero, 1)
            pool.wait_ge(s_w, 64)
            for c in range(KD):
                for w in (w_loops[:, c, c * P:(c + 1) * P], w_loops[:, c, D + c * P:D + (c + 1) * P],
                          w_l1[:, c, c * P:(c + 1) * P]):
                    last = pool.tensor_tensor(w, w, ident[:], ALU.add)
            last.then_inc(s_w_plus, 1)

            def gather(L, table, width):
                pool.wait_ge(s_passes, 1)
                n_pass = pool.value_load(passes_i[0:1, 0:1], min_val=1, max_val=MAXPASS)
                with pool.Fori(0, n_pass) as p:
                    with pool.Fori(0, ITERS) as it:
                        for s in range(SLOTS):
                            g = it * SLOTS + s
                            pool.wait_ge(L.staged, p * STAGES + g + 1)
                            pool.wait_ge(L.summed, p * NG + g + 1)
                            pool.sem_inc(L.allowed, 1)
                            for k in range(GT):
                                pool.indirect_dma_start(
                                    out=rows[:, s, k, 0:width], out_offset=None, in_=table,
                                    in_offset=bass.IndirectOffsetOnAxis(ap=idx_slot[s][:, k:k + 1], axis=0),
                                ).then_inc(L.gathered[s], 16)

            pool.wait_ge(s_t0[0], 16 * ((NT + 1) // 2))
            pool.wait_ge(s_t0[1], 16 * (NT // 2))
            gather(L0, table0, ROW0)

            pool.wait_ge(s_acc, NT)
            pool.memset(sums[:, 0:KD, :], 0.0).then_inc(s_rezero, 1)
            pool.wait_ge(s_t1[0], 16 * ((NT + 1) // 2))
            pool.wait_ge(s_t1[1], 16 * (NT // 2))
            gather(L1, table1, D)

        @block.scalar
        def _(act):
            def first_copy_in(T, u):
                free_of(act, s_xt, T)
                nc.scalar.copy(xs[:, u, :], x_sb[:, bass.ds(T, 1), :].rearrange("p t f -> p (t f)")
                               ).then_inc(s_xs, 1)

            def first(T, u, before):
                if not known(T, lambda t: t == NT - 1):
                    first_copy_in(T + 1, 1 - u)
                act.wait_ge(s_xt, T + 1)
                free_of(act, s_tab_ps, T)
                free_of(act, s_xT, T)
                nc.scalar.copy(xTs[:, u, :, :].rearrange("p c n -> p (c n)"), ps[6 + u][:, 0:D]).then_inc(s_xTs, 1)

            act.wait_ge(s_x, 32)
            first_copy_in(0, 0)
            over_tiles(act, first)

            def stage(L, s, g):
                nc.scalar.copy(idx_slot[s][:], idx_tab[:, bass.ds(g * GT, GT)])
                nc.scalar.copy(tab_slot[:, s, :, :], tabs[:, :, bass.ds(g * GT, GT)]).then_inc(L.staged, 1)

            act.wait_ge(s_passes, 1)
            n_pass = act.value_load(passes_i[0:1, 0:1], min_val=1, max_val=MAXPASS)
            with act.Fori(0, n_pass) as p:
                act.wait_ge(L0.base, p + 1)
                stage(L0, 0, 0)
                stage(L0, 1, 1)
                with act.Fori(0, ITERS) as it:
                    for s in range(SLOTS):
                        g = it * SLOTS + s
                        act.wait_ge(L0.summed, p * NG + g + SLOTS - 1)
                        stage(L0, (s + LOOK) % SLOTS, g + LOOK)
                        act.wait_ge(L0.staged, p * STAGES + g + 1)
                        for k in range(GT):
                            nc.scalar.activation(hot_rel[:, s % 2, k, 0:R], iota[:, 0:R], ACT.Abs,
                                                 bias=tab_slot[:, s, 2, k:k + 1])
                        act.drain()
                        nc.scalar.activation(hot_rel[:, s % 2, :, 0:R], hot_rel[:, s % 2, :, 0:R], ACT.Relu,
                                             bias=ones[:, 0:1], scale=-1.0).then_inc(L0.hot_rel, 1)
                        act.wait_ge(L0.score, p * NG + g + 1)
                        nc.scalar.activation(sc[:, s % 2, 2, :], sc[:, s % 2, 1, :], ACT.Exp).then_inc(L0.alpha, 1)
                        act.wait_ge(L0.hot_dst, p * NG + g + 1)
                        nc.scalar.copy(hot_dst_b[:, s % 2, :, :], hot_dst[:, s % 2, :, :]).then_inc(L0.hot_dst_b, 1)

            def copy_sums(T, u):
                free_of(act, s_agg, T)
                nc.scalar.copy(xTs[:, u, :, :], xT[:, :, tile_cols(T)])
                nc.scalar.copy(acc_s[:, u, :, :], sums[:, :, tile_cols(T)]).then_inc(s_acc, 1)

            def loop_message(T, u):
                act.wait_ge(s_mask, T + 1)
                nc.scalar.activation(yb[:, u, 0, :], ps[2 + u][:, 0:D], ACT.Identity, scale=col[:, u, 0:1]
                                     ).then_inc(s_loopm, 1)

            def deviation(T, u):
                act.wait_ge(s_var, T + 1)
                nc.scalar.activation(col[:, u, 3:4], mv[:, u, 1:2], ACT.Sqrt, bias=eps_t[:]).then_inc(s_std, 1)

            def middle(T, u, before):
                act.wait_ge(s_rstd, T + 1)
                nc.scalar.activation(x1s[:, u, :], yb[:, u, 2, :], ACT.Identity, bias=col[:, u, 5:6],
                                     scale=col[:, u, 4:5]).then_inc(s_x1, 1)
                if not known(T, lambda t: t + 1 >= NT):
                    loop_message(T + 1, 1 - u)
                act.wait_ge(s_x1t, T + 1)
                free_of(act, s_l1, T)
                nc.scalar.copy(x1Ts[:, u, :], ps[4 + u][:, 0:D]).then_inc(s_x1T, 1)
                if not known(T, lambda t: t + 1 >= NT):
                    deviation(T + 1, 1 - u)
                if not known(T, lambda t: t + 3 >= NT):
                    copy_sums(T + 3, 1 - u)
                act.wait_ge(s_l1, T + 1)
                free_of(act, s_sparse, T)
                nc.scalar.copy(hn[:, u, :], ps[6 + u][:, D:2 * D]).then_inc(s_hn, 1)
                nc.scalar.copy(x_sb[:, bass.ds(T, 1), :].rearrange("p t f -> p (t f)"), ps[6 + u][:, 0:D]
                               ).then_inc(s_res, 1)

            act.wait_ge(L0.added, n_pass * (NG + 1) + 1)
            copy_sums(0, 0)
            copy_sums(1, 1)
            loop_message(0, 0)
            copy_sums(2, 0)
            deviation(0, 0)
            over_tiles(act, middle)

            with act.Fori(0, n_pass) as p:
                act.wait_ge(L1.base, p + 1)
                stage(L1, 0, 0)
                stage(L1, 1, 1)
                with act.Fori(0, ITERS) as it:
                    for s in range(SLOTS):
                        g = it * SLOTS + s
                        act.wait_ge(L1.summed, p * NG + g + SLOTS - 1)
                        stage(L1, (s + LOOK) % SLOTS, g + LOOK)

            def copy_last(T, u):
                free_of(act, s_fagg, T)
                nc.scalar.copy(acc_s[:, u, 0:KD, :], sums[:, 0:KD, tile_cols(T)]).then_inc(s_facc, 1)

            def last(T, u, before):
                act.wait_ge(s_fvar, T + 1)
                nc.scalar.activation(col[:, u, 3:4], mv[:, u, 1:2], ACT.Sqrt, bias=eps_t[:]).then_inc(s_fstd, 1)
                if not known(T, lambda t: t + 2 >= NT):
                    copy_last(T + 2, u)
                act.wait_ge(s_frstd, T + 1)
                if not known(T, lambda t: t < 2):
                    act.wait_ge(s_out[u], 16 * before)
                nc.scalar.activation(x1s[:, u, :], yb[:, u, 2, :], ACT.Identity, bias=col[:, u, 5:6],
                                     scale=col[:, u, 4:5]).then_inc(s_fout, 1)

            act.wait_ge(L1.added, n_pass * (NG + 1) + 1)
            copy_last(0, 0)
            copy_last(1, 1)
            over_tiles(act, last)

        @block.tensor
        def _(pe):
            pe.wait_ge(s_ident, 2)
            pe.wait_ge(s_edge_f, 1)
            for k in range(3):
                for c in range(RC):
                    last = nc.tensor.transpose(ps[k][:, c * RP:(c + 1) * RP], edge_f[:, k, c, :], ident[0:RP, 0:RP])
            last.then_inc(s_edge_t, 1)
            pe.wait_ge(s_rel, 32)
            for r in range(2):
                for c in range(KD):
                    last = nc.tensor.transpose(ps[3][:, (2 * c + r) * P:(2 * c + r + 1) * P],
                                               rel_sb[:, r, c * P:(c + 1) * P], ident[:])
            last.then_inc(s_relT, 1)
            pe.wait_ge(s_relT_sb, 1)
            pe.wait_ge(s_wn, 16)
            for r in range(2):
                for c in range(KD):
                    last = nc.tensor.matmul(ps[4][:, r * D:(r + 1) * D], relT[:, c, r * P:(r + 1) * P],
                                            w_tab[:, c, 0:D], start=(c == 0), stop=(c == KD - 1))
            pe.wait_ge(s_wvec, 1)
            for c in range(KD):
                last = nc.tensor.matmul(ps[5][:, 0:R], wr_bc[:, c, :], relT[:, c, 0:R],
                                        start=(c == 0), stop=(c == KD - 1))
            last.then_inc(s_relp, 1)

            def transpose_x(T, u):
                pe.wait_ge(s_xs, T + 1)
                free_of(pe, s_xTs, T)
                for c in range(KD):
                    last = nc.tensor.transpose(ps[6 + u][:, c * P:(c + 1) * P], xs[:, u, c * P:(c + 1) * P], ident[:])
                last.then_inc(s_xt, 1)

            def first(T, u, before):
                if not known(T, lambda t: t == NT - 1):
                    transpose_x(T + 1, 1 - u)
                pe.wait_ge(s_xTs, T + 1)
                free_of(pe, s_tab_sb, T)
                for c in range(KD):
                    nc.tensor.matmul(ps[0 + u][:, 0:D + 1], xTs[:, u, c, :], w_tab[:, c, :],
                                     start=(c == 0), stop=(c == KD - 1))
                for c in range(KD):
                    last = nc.tensor.matmul(ps[2 + u][:, 0:P], wd_bc[:, c, :], xTs[:, u, c, :],
                                            start=(c == 0), stop=(c == KD - 1))
                last.then_inc(s_tab_ps, 1)

            pe.wait_ge(s_setup, 1)
            transpose_x(0, 0)
            over_tiles(pe, first)

            pe.sem_inc(L0.summed, SLOTS)
            pe.sem_inc(L1.summed, SLOTS)
            pe.wait_ge(s_passes, 1)
            n_pass = pe.value_load(passes_i[0:1, 0:1], min_val=1, max_val=MAXPASS)
            with pe.Fori(0, n_pass) as p:
                with pe.Fori(0, ITERS) as it:
                    for s in range(SLOTS):
                        g = it * SLOTS + s
                        pe.wait_ge(L0.added, p * (NG + 1) + g + 1)
                        pe.wait_ge(L0.hot_dst, p * NG + g + 1)
                        for q in range(KD):
                            for k in range(GT):
                                nc.tensor.matmul(ps[s % 2][:, q * P:(q + 1) * P], rows[:, s, k, q * P:(q + 1) * P],
                                                 hot_dst[:, s % 2, k, :], start=(k == 0), stop=(k == GT - 1))
                        pe.wait_ge(L0.hot_rel, p * NG + g + 1)
                        pe.wait_ge(L0.hot_dst_b, p * NG + g + 1)
                        for r in range(2):
                            for k in range(GT):
                                last = nc.tensor.matmul(ps[s % 2][:, (KD + r) * P:(KD + r + 1) * P],
                                                        hot_rel[:, s % 2, k, r * P:(r + 1) * P],
                                                        hot_dst_b[:, s % 2, k, :], start=(k == 0), stop=(k == GT - 1))
                        last.then_inc(L0.summed, 1)

            def node_products(T, u):
                pe.wait_ge(s_acc, T + 1)
                if not known(T, lambda t: t < 2):
                    pe.wait_ge(s_joined, T - 1)
                for r in range(2):
                    nc.tensor.matmul(ps[0 + u][:, 0:D + 1], acc_s[:, u, KD + r, :], rel_tab[:, r, :],
                                     start=(r == 0), stop=False)
                for c in range(KD):
                    nc.tensor.matmul(ps[0 + u][:, c * P:(c + 1) * P], acc_s[:, u, c, :], ident[:],
                                     start=False, stop=(c == KD - 1))
                for c in range(KD):
                    last = nc.tensor.matmul(ps[2 + u][:, :], xTs[:, u, c, :], w_loops[:, c, :],
                                            start=(c == 0), stop=(c == KD - 1))
                last.then_inc(s_agg, 1)

            def middle(T, u, before):
                pe.wait_ge(s_x1, T + 1)
                free_of(pe, s_x1T, T)
                for c in range(KD):
                    last = nc.tensor.transpose(ps[4 + u][:, c * P:(c + 1) * P], x1s[:, u, c * P:(c + 1) * P], ident[:])
                last.then_inc(s_x1t, 1)
                if not known(T, lambda t: t + 2 >= NT):
                    node_products(T + 2, u)
                pe.wait_ge(s_x1T, T + 1)
                free_of(pe, s_res, T)
                for c in range(KD):
                    last = nc.tensor.matmul(ps[6 + u][:, :], x1Ts[:, u, c * P:(c + 1) * P], w_l1[:, c, :],
                                            start=(c == 0), stop=(c == KD - 1))
                last.then_inc(s_l1, 1)

            pe.wait_ge(s_w_plus, 1)
            node_products(0, 0)
            node_products(1, 1)
            over_tiles(pe, middle)

            pe.wait_ge(s_joined, NT)
            with pe.Fori(0, n_pass) as p:
                with pe.Fori(0, ITERS) as it:
                    for s in range(SLOTS):
                        g = it * SLOTS + s
                        pe.wait_ge(L1.added, p * (NG + 1) + g + 1)
                        pe.wait_ge(L1.hot_dst, p * NG + g + 1)
                        pe.wait_ge(L1.gathered[s], (p * ITERS + it + 1) * GT * 16)
                        for q in range(KD):
                            for k in range(GT):
                                last = nc.tensor.matmul(ps[s % 2][:, q * P:(q + 1) * P],
                                                        rows[:, s, k, q * P:(q + 1) * P], hot_dst[:, s % 2, k, :],
                                                        start=(k == 0), stop=(k == GT - 1))
                        last.then_inc(L1.summed, 1)

            def last_rows(T, u, before):
                pe.wait_ge(s_facc, T + 1)
                free_of(pe, s_fvar, T)
                for c in range(KD):
                    last = nc.tensor.transpose(ps[2 + u][:, c * P:(c + 1) * P], acc_s[:, u, c, :], ident[:])
                last.then_inc(s_fagg, 1)
            over_tiles(pe, last_rows)

        @block.vector
        def _(dve):
            V = nc.vector

            def settle():
                dve.drain()

            V.memset(ones[:], 1.0)
            V.memset(eps_t[:], EPS)
            V.memset(tabs[:], 0.0)
            V.memset(idx_tab[:], 0)
            V.memset(tab_out[:], 0.0)
            V.memset(base_i[:], 0)
            dve.wait_ge(s_ones, 1)
            V.tensor_copy(iota[:], iota_i)
            dve.wait_ge(s_edges, 9 * 16)
            V.tensor_copy(edge_f[:, :, :, :].rearrange("r k c i -> r k (c i)"),
                          edge_rows[:, :, :, :].rearrange("r k c i -> r k (c i)")).then_inc(s_edge_f, 1)
            dve.wait_ge(s_w3, 32)
            for c in range(6):
                V.tensor_tensor_reduce(out=w3_sb[:, c, :], in0=w3_sb[:, c, :], in1=a_bc, scale=1.0, scalar=0.0,
                                       op0=ALU.mult, op1=ALU.add, accum_out=w_vec[:, c:c + 1])
            settle()
            V.tensor_copy(w_tab[:, :, D:D + 1].rearrange("p c o -> p (c o)"), w_vec[:, 0:2])
            for c in range(KD):
                V.tensor_scalar(wd_bc[:, c, :], ones[:], w_vec[:, 2 + c:3 + c], None, ALU.mult)
                last = V.tensor_scalar(wr_bc[:, c, :], ones[:], w_vec[:, 4 + c:5 + c], None, ALU.mult)
            last.then_inc(s_wvec, 1)
            dve.wait_ge(s_edge_t, 1)
            V.tensor_copy(dst_f[:], ps[0][:, 0:NE])
            V.tensor_copy(idx_tab[:, 0:NE], ps[1][:, 0:NE])
            V.tensor_copy(tabs[:, 1, 0:NE], ps[2][:, 0:NE])
            V.tensor_scalar(tabs[:, 2, 0:NE], ps[2][:, 0:NE], -1.0, None, ALU.mult)
            V.memset(hot_rel[:, :, :, R:256], 0.0)
            settle()
            V.tensor_reduce(span_in[:, 1, :], dst_f[:].rearrange("p (g k) -> p g k", k=GT), AX.X, ALU.max)
            V.tensor_reduce(base_cur[:], dst_f[:].rearrange("p (g k) -> p g k", k=GT), AX.X, ALU.min)
            settle()
            V.tensor_scalar(span_in[:, 0, :], base_cur[:], -1.0, None, ALU.mult).then_inc(s_span, 1)
            dve.wait_ge(s_relT, 1)
            V.tensor_copy(relT.rearrange("p c r -> p (c r)"), ps[3][:, :]).then_inc(s_relT_sb, 1)
            dve.wait_ge(s_relp, 1)
            V.tensor_copy(rel_tab[:, :, 0:D], ps[4][:, :].rearrange("p (r f) -> p r f", r=2))
            V.memset(rel_tab[:, :, D:D + 1], 1.0)
            V.tensor_copy(rel_score[:], ps[5][:, 0:R]).then_inc(s_setup, 1)
            dve.wait_ge(s_spanned, 1)
            V.tensor_tensor(base_cur[:], span[:, 0, :], span[:, 1, :], ALU.add)
            settle()
            V.reduce_max(flags[:, 0:1], base_cur[:], AX.X)
            settle()
            V.tensor_scalar(flags[:, 1:2], flags[:, 0:1], float(P), None, ALU.is_ge)
            V.tensor_scalar(flags[:, 2:3], flags[:, 0:1], float(P), None, ALU.is_lt)
            settle()
            V.tensor_scalar(passes_i[:], flags[:, 1:2], float(MAXPASS - 1), 1.0, ALU.mult, ALU.add)
            V.tensor_scalar(base0[:], span[:, 0, :], flags[:, 2:3], -1.0, ALU.mult, ALU.mult)
            settle()
            V.sem_inc(s_passes, 1)

            def first(T, u, before):
                dve.wait_ge(s_xTs, T + 1)
                V.tensor_copy(xT[:, :, tile_cols(T)], xTs[:, u, :, :]).then_inc(s_xT, 1)
                dve.wait_ge(s_tab_ps, T + 1)
                if not known(T, lambda t: t < 2):
                    dve.wait_ge(s_t0[u], before * 16)
                V.tensor_copy(tab_out[:, u, 0:D + 1], ps[0 + u][:, 0:D + 1])
                V.tensor_copy(dst_score[:, tile_cols(T)], ps[2 + u][:, 0:P]).then_inc(s_tab_sb, 1)
            over_tiles(dve, first)

            dve.wait_ge(s_zero, 2)
            dve.sem_inc(L0.added, 1)
            dve.sem_inc(L1.added, 1)
            n_pass = dve.value_load(passes_i[0:1, 0:1], min_val=1, max_val=MAXPASS)

            def begin_layer():
                V.tensor_copy(base_cur[:], base0[:])
                settle()

            def begin_pass(L, width):
                V.tensor_copy(base_i[:, 1:1 + NG], base_cur[:])
                V.memset(ps[1][:, 0:width * P], 0.0)
                V.tensor_tensor(tabs[:, 0, 0:NE].rearrange("p (g k) -> p g k", k=GT),
                                dst_f[:].rearrange("p (g k) -> p g k", k=GT),
                                base_cur[:].unsqueeze(2).broadcast_to([P, NG, GT]), ALU.subtract)
                settle()
                dve.sem_inc(L.base, 1)

            def add_window(L, p, g, s, width):
                base = dve.value_load(base_i[0:1, bass.ds(g, 1)], min_val=0, max_val=N)
                dve.wait_ge(L.added, p * (NG + 1) + g + 1)
                dve.wait_ge(L.summed, p * NG + g + SLOTS)
                win = sums[:, 0:width, bass.ds(base, P)]
                V.tensor_tensor(win, win, ps[(s + 1) % 2][:, 0:width * P].rearrange("p (q n) -> p q n", n=P),
                                ALU.add).then_inc(L.added, 1)

            def end_pass(L, p):
                dve.wait_ge(L.staged, (p + 1) * STAGES)
                V.tensor_scalar(base_cur[:], base_cur[:], float(P), None, ALU.add)
                settle()

            begin_layer()
            with dve.Fori(0, n_pass) as p:
                begin_pass(L0, 4)
                with dve.Fori(0, ITERS) as it:
                    for s in range(SLOTS):
                        g = it * SLOTS + s
                        b = s % 2
                        base = dve.value_load(base_i[0:1, bass.ds(g + 1, 1)], min_val=0, max_val=N)
                        dve.wait_ge(L0.staged, p * STAGES + g + 1)
                        dve.wait_ge(L0.summed, p * NG + g + SLOTS - 1)
                        for k in range(GT):
                            V.scalar_tensor_tensor(out=hot_dst[:, b, k, :], in0=iota[:, 0:P],
                                                   scalar=tab_slot[:, s, 0, k:k + 1],
                                                   in1=dst_score[:, bass.ds(base, P)], op0=ALU.is_equal,
                                                   op1=ALU.mult, accum_out=score_dst[:, b, k:k + 1])
                        for k in range(GT):
                            V.scalar_tensor_tensor(out=products[:, k, :], in0=iota[:, 0:R],
                                                   scalar=tab_slot[:, s, 1, k:k + 1], in1=rel_score[:],
                                                   op0=ALU.is_equal, op1=ALU.mult,
                                                   accum_out=score_rel[:, b, k:k + 1])
                        settle()
                        V.tensor_tensor(sc[:, b, 0, :], score_dst[:, b, :], score_rel[:, b, :], ALU.add)
                        settle()
                        dve.wait_ge(L0.gathered[s], (p * ITERS + it + 1) * GT * 16)
                        V.tensor_tensor(sc[:, b, 0, :], sc[:, b, 0, :], rows[:, s, :, D], ALU.add)
                        settle()
                        V.scalar_tensor_tensor(out=sc[:, b, 1, :], in0=sc[:, b, 0, :], scalar=0.01,
                                               in1=sc[:, b, 0, :], op0=ALU.mult, op1=ALU.max).then_inc(L0.score, 1)
                        dve.wait_ge(L0.alpha, p * NG + g + 1)
                        V.tensor_scalar(sc[:, b, 3, :], sc[:, b, 2, :], 0.25, None, ALU.mult)
                        settle()
                        V.reciprocal(sc[:, b, 4, :], sc[:, b, 3, :])
                        settle()
                        V.tensor_tensor(sc[:, b, 5, :], sc[:, b, 3, :], sc[:, b, 4, :], ALU.mult)
                        settle()
                        for k in range(GT):
                            last = V.tensor_scalar(hot_dst[:, b, k, :], iota[:, 0:P], tab_slot[:, s, 0, k:k + 1],
                                                   sc[:, b, 5, k:k + 1], ALU.is_equal, ALU.mult)
                        last.then_inc(L0.hot_dst, 1)
                        add_window(L0, p, g, s, 4)
                add_window(L0, p, NG, NG, 4)
                end_pass(L0, p)

            def node_step(T, u, top_T, top_u, top_before):
                join, top = T is not None, top_T is not None
                if join:
                    dve.wait_ge(s_agg, T + 1)
                if top:
                    dve.wait_ge(s_hn, top_T + 1)

                def top_round(r, half):
                    source = hn[:, top_u, :] if r == 0 else work[:, top_u, :]
                    if top and half == 0:
                        V.max(top8[:, top_u, :], source)
                    elif top:
                        V.match_replace(work[:, top_u, :], top8[:, top_u, :], source, LOWEST)

                if join:
                    count = ps[0 + u][:, D:D + 1]
                    V.tensor_scalar(col[:, u, 0:1], count, 0.0, None, ALU.is_gt)
                    V.tensor_scalar(col[:, u, 1:2], count, 0.0, None, ALU.is_le)
                    V.tensor_scalar(col[:, u, 2:3], count, 1.0, None, ALU.max)
                top_round(0, 0)
                settle()
                if join:
                    V.reciprocal(r_deg[:, bass.ds(T, 1)], col[:, u, 2:3]).then_inc(s_mask, 1)
                top_round(0, 1)
                settle()
                if join:
                    dve.wait_ge(s_loopm, T + 1)
                    V.scalar_tensor_tensor(out=yb[:, u, 1, :], in0=ps[2 + u][:, D:2 * D], scalar=col[:, u, 1:2],
                                           in1=yb[:, u, 0, :], op0=ALU.mult, op1=ALU.add)
                top_round(1, 0)
                settle()
                if join:
                    V.scalar_tensor_tensor(out=yb[:, u, 2, :], in0=ps[0 + u][:, 0:D], scalar=0.0,
                                           in1=yb[:, u, 1, :], op0=ALU.max, op1=ALU.add).then_inc(s_joined, 1)
                top_round(1, 1)
                settle()
                if join:
                    V.bn_stats(bn[:, u, :], yb[:, u, 2, :])
                top_round(2, 0)
                settle()
                if join:
                    V.bn_aggr(mv[:, u, :], bn[:, u, :]).then_inc(s_var, 1)
                top_round(2, 1)
                settle()
                for r in range(3, TOPK // 8):
                    top_round(r, 0)
                    if top:
                        settle()
                    top_round(r, 1)
                    if top:
                        settle()
                if top:
                    if not known(top_T, lambda t: t < 2):
                        dve.wait_ge(s_t1[top_u], top_before * 16)
                    V.scalar_tensor_tensor(out=sparse[:, top_u, :], in0=work[:, top_u, :], scalar=LOWEST,
                                           in1=hn[:, top_u, :], op0=ALU.is_equal, op1=ALU.mult
                                           ).then_inc(s_sparse, 1)

            def middle(T, u, before):
                dve.wait_ge(s_std, T + 1)
                V.reciprocal(col[:, u, 4:5], col[:, u, 3:4])
                settle()
                V.tensor_scalar(col[:, u, 5:6], mv[:, u, 0:1], col[:, u, 4:5], -1.0, ALU.mult,
                                ALU.mult).then_inc(s_rstd, 1)
                node_step(None if known(T, lambda t: t == NT - 1) else T + 1, 1 - u,
                          None if known(T, lambda t: t == 0) else T - 1, 1 - u, before if u else before - 1)

            node_step(0, 0, None, None, None)
            over_tiles(dve, middle)
            node_step(None, None, NT - 1, 0, NT // 2)

            begin_layer()
            dve.wait_ge(s_rezero, 1)
            with dve.Fori(0, n_pass) as p:
                begin_pass(L1, KD)
                with dve.Fori(0, ITERS) as it:
                    for s in range(SLOTS):
                        g = it * SLOTS + s
                        dve.wait_ge(L1.staged, p * STAGES + g + 1)
                        dve.wait_ge(L1.summed, p * NG + g + SLOTS - 1)
                        V.tensor_tensor(hot_dst[:, s % 2, :, :], iota[:, 0:P].unsqueeze(1).broadcast_to([P, GT, P]),
                                        tab_slot[:, s, 0, :].unsqueeze(2).broadcast_to([P, GT, P]),
                                        ALU.is_equal).then_inc(L1.hot_dst, 1)
                        add_window(L1, p, g, s, KD)
                add_window(L1, p, NG, NG, KD)
                end_pass(L1, p)

            def last(T, u, before):
                dve.wait_ge(s_fagg, T + 1)
                free_of(dve, s_fout, T)
                V.scalar_tensor_tensor(out=yb[:, u, 2, :], in0=ps[2 + u][:, 0:D], scalar=r_deg[:, bass.ds(T, 1)],
                                       in1=x_sb[:, bass.ds(T, 1), :].rearrange("p t f -> p (t f)"),
                                       op0=ALU.mult, op1=ALU.add)
                settle()
                V.bn_stats(bn[:, u, :], yb[:, u, 2, :])
                settle()
                V.bn_aggr(mv[:, u, :], bn[:, u, :]).then_inc(s_fvar, 1)
                if not known(T, lambda t: t == 0):
                    normalise(T - 1, 1 - u)

            def normalise(T, u):
                dve.wait_ge(s_fstd, T + 1)
                V.reciprocal(col[:, u, 4:5], col[:, u, 3:4])
                settle()
                V.tensor_scalar(col[:, u, 5:6], mv[:, u, 0:1], col[:, u, 4:5], -1.0, ALU.mult,
                                ALU.mult).then_inc(s_frstd, 1)
            over_tiles(dve, last)
            normalise(NT - 1, 0)


_INS = ["x", "src", "dst", "edge_type_200", "L0_gnn_rel_emb", "L0_gnn_weight_neighbor", "L0_gnn_a", "L0_gnn_W3",
        "L0_gnn_loop_weight", "L0_gnn_evolve_loop_weight", "L1_gnn_W_self", "L1_gnn_W_neigh"]


def kernel(**inputs):
    import numpy as _np
    import concourse.bacc as _bacc
    from concourse import mybir as _mybir
    from concourse.bass_utils import run_bass_kernel_spmd as _run

    nc = _bacc.Bacc("TRN2", target_bir_lowering=False, num_devices=1)
    arrays, args = {}, []
    for name in _INS:
        arr = _np.ascontiguousarray(inputs[name])
        arrays[f"in_{name}_dram"] = arr
        args.append(nc.dram_tensor(f"in_{name}_dram", arr.shape, _mybir.dt.from_np(arr.dtype),
                                   kind="ExternalInput").ap())
    args.append(nc.dram_tensor("out_0_dram", tuple(inputs["x"].shape), _mybir.dt.float32,
                               kind="ExternalOutput").ap())
    gnn_two_layers(nc, *args)
    r = _run(nc, [arrays], core_ids=[0])
    return r.results[0]["out_0_dram"]
```

```python
from contextlib import ExitStack

import concourse.bass as bass
from concourse import mybir



def gnn_two_layers(nc, x, src, dst, etype, rel_emb, w_neighbor, a, w3, loop_w, evolve_w, w_self, w_neigh, out):
    f32, i32, bf16 = mybir.dt.float32, mybir.dt.int32, mybir.dt.bfloat16
    ALU, ACT, AX = mybir.AluOpType, mybir.ActivationFunctionType, mybir.AxisListType
    RMAX = bass.bass_isa.ReduceOp.max

    P = 128
    N, D = x.shape
    E = src.shape[0]
    R = rel_emb.shape[0]
    KD = D // P
    NT = -(-N // P)
    TAIL = N - (NT - 1) * P
    NPAD = NT * P
    EFULL = E // P
    EREM = E - EFULL * P
    GT = 8
    SLOTS = 4
    NG = -(-(EFULL + 1) // (GT * SLOTS)) * SLOTS
    ITERS = NG // SLOTS
    NE = NG * GT
    LOOK = 2
    RC = 4
    RP = NE // RC
    STAGES = NG + LOOK
    ROW0 = 272
    NACC = N + P
    TOPK = 32
    EPS = 1e-5
    LOWEST = -3.4028234663852886e38
    MAXPASS = NT
    X0 = 4
    SC = 512

    table0 = nc.dram_tensor("table0", (NPAD, ROW0), f32).ap()
    table1 = nc.dram_tensor("table1", (NPAD, D), f32).ap()

    ctx = ExitStack()
    with ctx:
        def sb(name, shape, dt=f32):
            return ctx.enter_context(nc.sbuf_tensor(name, shape, dt))

        def sem(name):
            return ctx.enter_context(nc.semaphore(name))

        ident = sb("ident", [P, P])
        iota = sb("iota", [P, 256])
        ones = sb("ones", [P, P])
        eps_t = sb("eps_t", [P, 1])
        x_sb = sb("x_sb", [P, NT, D])
        xT = sb("xT", [P, KD, NPAD])
        sums = sb("sums", [P, 4, NACC])
        dst_score = sb("dst_score", [P, NACC])
        rel_score = sb("rel_score", [P, R])
        rows = sb("rows", [P, SLOTS, GT, ROW0])
        hot_dst = sb("hot_dst", [P, 2, GT, P])
        hot_dst_b = sb("hot_dst_b", [P, 2, GT, P], bf16)
        hot_rel = sb("hot_rel", [P, 2, GT, 256], bf16)
        w_tab = sb("w_tab", [P, KD, D + 1])
        w_loops = sb("w_loops", [P, KD, 2 * D])
        w_l1 = sb("w_l1", [P, KD, 2 * D])
        w_vec = sb("w_vec", [P, 6])
        wd_bc = sb("wd_bc", [P, KD, P])
        rel_tab = sb("rel_tab", [P, 2, D + 1])
        tabs = sb("tabs", [P, 3, STAGES * GT])
        dst_f = sb("dst_f", [P, NE])
        idx_tab = sb("idx_tab", [P, STAGES * GT], i32)
        tab_slot = sb("tab_slot", [P, SLOTS, 3, GT])
        idx_slot = [sb(f"idx_slot{s}", [P, GT], i32) for s in range(SLOTS)]
        span_in = sb("span_in", [P, 2, NG])
        span = sb("span", [P, 2, NG])
        base0 = sb("base0", [P, NG])
        base_cur = sb("base_cur", [P, NG])
        base_i = sb("base_i", [P, 2 + NG], i32)
        flags = sb("flags", [P, 8])
        passes_i = sb("passes_i", [P, 1], i32)
        score_dst = sb("score_dst", [P, 2, GT])
        score_rel = sb("score_rel", [P, 2, GT])
        sc = sb("sc", [P, 2, 6, GT])
        r_deg = sb("r_deg", [P, NT])
        node_slots = sb("node_slots", [P, 4, D])
        xs = node_slots[:, 0:2, :]
        xTs = node_slots[:, 2:4, :].rearrange("p u (c n) -> p u c n", c=KD)
        products_r = node_slots[:].rearrange("p a f -> p (a f)")[:, 0:GT * R // 2].bitcast(bf16).rearrange(
            "p (k r) -> p k r", k=GT)
        tab_out = sb("tab_out", [P, 4, ROW0])
        products_d = tab_out[:].rearrange("p u w -> p (u w)")[:, 0:GT * P // 2].bitcast(bf16).rearrange(
            "p (k n) -> p k n", k=GT)
        col = sb("col", [P, 2, 8])
        bn = sb("bn", [P, 2, 6])
        mv = sb("mv", [P, 2, 2])
        a_bc = hot_dst[:, 0, :, :].rearrange("p k n -> p (k n)")[:, 0:3 * D]
        rows_flat = rows[:].rearrange("p s k w -> p (s k w)")
        flat_used = [0]

        def in_rows(*shape):
            n = 1
            for d in shape:
                n *= d
            at = flat_used[0]
            flat_used[0] += n
            assert flat_used[0] <= SLOTS * GT * ROW0
            names = "abcd"[:len(shape)]
            return rows_flat[:, at:at + n].rearrange(f"p ({' '.join(names)}) -> p {' '.join(names)}",
                                                     **dict(zip(names, shape)))

        w3_first = in_rows(KD, 3 * D)
        iota_i = in_rows(256).bitcast(i32)
        flat_used[0] = GT * ROW0
        edge_rows = in_rows(3, RC, P).bitcast(i32)[0:RP]
        flat_used[0] = 2 * GT * ROW0
        w3_rest = in_rows(6 - KD, 3 * D)
        rel_sb = in_rows(2, D)
        relT = in_rows(KD, 256)
        wr_bc = in_rows(KD, P)
        flat_used[0] = 0
        x1Ts = in_rows(2, D)
        acc_s = in_rows(2, 4, P)
        yb = in_rows(2, 4, D)
        x1s = in_rows(2, D)
        hn = in_rows(2, D)
        work = in_rows(2, D)
        sparse = in_rows(2, D)
        outs = in_rows(4, D)
        edge_f = hot_rel[:].rearrange("p s k w -> p (s k w)").bitcast(f32)[0:RP, 0:3 * RC * P].rearrange(
            "p (a c i) -> p a c i", a=3, c=RC)
        top8 = sb("top8", [P, 2, 8])

        ps = [ctx.enter_context(nc.psum_tensor(f"ps{b}", [P, 512], f32)) for b in range(8)]

        s_ident = sem("s_ident")
        s_pads = sem("s_pads")
        s_ones = sem("s_ones")
        s_edges = sem("s_edges")
        s_rel = sem("s_rel")
        s_w3 = sem("s_w3")
        s_wn = sem("s_wn")
        s_x = [sem(f"s_x_load{c}") for c in range(3)]
        s_wa = sem("s_wa")
        s_wsrc = sem("s_wsrc")
        s_w3a = sem("s_w3a")
        s_dscore = sem("s_dscore")
        s_dscore_sb = sem("s_dscore_sb")
        s_w = sem("s_w")
        s_w_plus = sem("s_w_plus")
        s_zero = sem("s_zero")
        s_edge_f = sem("s_edge_f")
        s_edge_t = sem("s_edge_t")
        s_span = sem("s_span")
        s_spanned = sem("s_spanned")
        s_passes = sem("s_passes")
        s_wvec = sem("s_wvec")
        s_relT = sem("s_relT")
        s_relT_sb = sem("s_relT_sb")
        s_relp = sem("s_relp")
        s_setup = sem("s_setup")
        s_xs = sem("s_xs")
        s_xt = sem("s_xt")
        s_xTs = sem("s_xTs")
        s_xT = sem("s_xT")
        s_tab_ps = sem("s_tab_ps")
        s_tab_sb = sem("s_tab_sb")
        s_t0 = [sem(f"s_t0_{f}") for f in range(4)]
        s_acc = sem("s_acc")
        s_agg = sem("s_agg")
        s_mask = sem("s_mask")
        s_parts = sem("s_parts")
        s_half = sem("s_half")
        s_joined = sem("s_joined")
        s_top = sem("s_top")
        s_var = sem("s_var")
        s_std = sem("s_std")
        s_rstd = sem("s_rstd")
        s_x1 = sem("s_x1")
        s_x1t = sem("s_x1t")
        s_x1T = sem("s_x1T")
        s_l1 = sem("s_l1")
        s_hn = sem("s_hn")
        s_res = sem("s_res")
        s_sparse = sem("s_sparse")
        s_t1 = [sem(f"s_t1_{u}") for u in range(2)]
        s_rezero = sem("s_rezero")
        s_facc = sem("s_facc")
        s_fagg = sem("s_fagg")
        s_fvar = sem("s_fvar")
        s_fstd = sem("s_fstd")
        s_frstd = sem("s_frstd")
        s_fout = sem("s_fout")
        s_out = [sem(f"s_out{f}") for f in range(4)]

        class Layer:
            def __init__(self, tag):
                self.base = sem(f"base_ready{tag}")
                self.staged = sem(f"staged{tag}")
                self.allowed = sem(f"allowed{tag}")
                self.gathered = [sem(f"gathered{tag}_{s}") for s in range(SLOTS)]
                self.hot_rel = sem(f"hot_rel{tag}")
                self.score = sem(f"score{tag}")
                self.alpha = sem(f"alpha{tag}")
                self.hot_dst = sem(f"hot_dst{tag}")
                self.hot_dst_b = sem(f"hot_dst_b{tag}")
                self.looked_up = sem(f"looked_up{tag}")
                self.joined = sem(f"joined{tag}")
                self.scored = sem(f"scored{tag}")
                self.quarter = sem(f"quarter{tag}")
                self.inverse = sem(f"inverse{tag}")
                self.weight = sem(f"weight{tag}")
                self.summed = sem(f"summed{tag}")
                self.added = sem(f"added{tag}")

        L0, L1 = Layer("0"), Layer("1")

        def over_tiles(eng, step):
            for T in range(4):
                step(T, T % 2, T // 2, T % 4, T // 4)
            with eng.Fori(0, (NT - 9) // 4) as it:
                for v in range(4):
                    step(it * 4 + 4 + v, v % 2, it * 2 + 2 + v // 2, v, it + 1)
            for T in range(NT - 5, NT):
                step(T, T % 2, T // 2, T % 4, T // 4)

        def known(T, test):
            return isinstance(T, int) and test(T)

        def free_of(eng, done, T):
            if not known(T, lambda t: t < 2):
                eng.wait_ge(done, T - 1)

        def tile_cols(T):
            return bass.ds(T * P, P)

        block = ctx.enter_context(nc.Block())

        @block.sync
        def _(sp):
            w3_rows = w3.rearrange("(c p) k -> p c k", p=P)
            x_tiles = x[0:(NT - 1) * P, :].rearrange("(t p) f -> p t f", p=P)
            sp.dma_start(w3_first, w3_rows[:, 0:KD, :]).then_inc(s_wa, 16)
            sp.dma_start(a_bc, a.rearrange("k o -> o k").broadcast_to([P, 3 * D])).then_inc(s_wa, 16)
            sp.dma_start(x_sb[:, 0:X0, :], x_tiles[:, 0:X0, :]).then_inc(s_x[0], 16)
            sp.dma_start(w_tab[:, :, 0:D], w_neighbor.rearrange("(c p) f -> p c f", p=P)).then_inc(s_wn, 16)
            sp.dma_start(x_sb[:, X0:NT - 1, :], x_tiles[:, X0:NT - 1, :]).then_inc(s_x[1], 16)
            sp.wait_ge(s_pads, 5)
            sp.dma_start(x_sb[0:TAIL, NT - 1, :], x[(NT - 1) * P:N, :]).then_inc(s_x[2], 16)
            sp.dma_start(w3_rest, w3_rows[:, KD:6, :]).then_inc(s_w3, 16)
            sp.dma_start(rel_sb[:, 0, :], rel_emb[0:P, :]).then_inc(s_rel, 16)
            sp.dma_start(rel_sb[0:R - P, 1, :], rel_emb[P:R, :]).then_inc(s_rel, 16)
            sp.dma_start(w_loops[:, :, 0:D], loop_w.rearrange("(c p) f -> p c f", p=P)).then_inc(s_w, 16)
            sp.dma_start(w_loops[:, :, D:2 * D], evolve_w.rearrange("(c p) f -> p c f", p=P)).then_inc(s_w, 16)
            sp.dma_start(w_l1[:, :, 0:D], w_self.rearrange("(c p) f -> p c f", p=P)).then_inc(s_w, 16)
            sp.dma_start(w_l1[:, :, D:2 * D], w_neigh.rearrange("(c p) f -> p c f", p=P)).then_inc(s_w, 16)

            def store_table0(T, u, before, f, before4):
                sp.wait_ge(s_tab_sb, T + 1)
                sp.dma_start(table0[tile_cols(T), :], tab_out[:, f, :]).then_inc(s_t0[f], 16)
            over_tiles(sp, store_table0)

            def store_table1(T, u, before, f, before4):
                sp.wait_ge(s_sparse, T + 1)
                sp.dma_start(table1[tile_cols(T), :], sparse[:, u, :]).then_inc(s_t1[u], 16)
            over_tiles(sp, store_table1)

            def store_out(T, u, before, f, before4):
                sp.wait_ge(s_fout, T + 1)
                if known(T, lambda t: t == NT - 1):
                    sp.dma_start(out[(NT - 1) * P:N, :], outs[0:TAIL, f, :]).then_inc(s_out[f], 16)
                else:
                    sp.dma_start(out[tile_cols(T), :], outs[:, f, :]).then_inc(s_out[f], 16)
            over_tiles(sp, store_out)
            for f in range(4):
                sp.wait_ge(s_out[f], 16 * len(range(f, NT, 4)))

        @block.gpsimd
        def _(pool):
            for k, pad in enumerate((N, 0, 0)):
                pool.memset(edge_rows[:, k, RC - 1, :], pad).then_inc(s_pads, 1)
            pool.memset(rel_sb, 0.0).then_inc(s_pads, 1)
            pool.memset(x_sb[:, NT - 1, :], 0.0).then_inc(s_pads, 1)
            pool.memset(ident[:], 0.0).then_inc(s_ident, 1)
            pool.iota(iota_i, pattern=[[1, 256]], base=0, channel_multiplier=0).then_inc(s_ones, 1)
            pool.wait_ge(s_ident, 1)
            pool.affine_select(out=ident[:], in_=ident[:], compare_op=ALU.not_equal, fill=1.0, base=0,
                               pattern=[[-1, P]], channel_multiplier=1).then_inc(s_ident, 1)
            pool.memset(dst_score[:, NPAD:NACC], 0.0).then_inc(s_zero, 1)
            pool.memset(sums[:], 0.0).then_inc(s_zero, 1)
            pool.wait_ge(s_wa, 32)
            pool.wait_ge(s_w3, 16)
            pool.tensor_tensor(w3_rest, w3_rest, a_bc.unsqueeze(1).broadcast_to([P, 6 - KD, 3 * D]),
                               ALU.mult).then_inc(s_w3a, 1)
            pool.wait_ge(s_span, 1)
            pool.partition_all_reduce(span[:].rearrange("p a g -> p (a g)"),
                                      span_in[:].rearrange("p a g -> p (a g)"), P, RMAX).then_inc(s_spanned, 1)
            pool.wait_ge(s_w, 64)
            for c in range(KD):
                for w in (w_loops[:, c, c * P:(c + 1) * P], w_loops[:, c, D + c * P:D + (c + 1) * P],
                          w_l1[:, c, c * P:(c + 1) * P]):
                    last = pool.tensor_tensor(w, w, ident[:], ALU.add)
            last.then_inc(s_w_plus, 1)

            def gather(L, table, width):
                pool.wait_ge(s_passes, 1)
                n_pass = pool.value_load(passes_i[0:1, 0:1], min_val=1, max_val=MAXPASS)
                with pool.Fori(0, n_pass) as p:
                    with pool.Fori(0, ITERS) as it:
                        for s in range(SLOTS):
                            g = it * SLOTS + s
                            if L is L0 and s == 2:
                                pool.wait_ge(s_setup, 1)
                            pool.wait_ge(L.staged, p * STAGES + g + 1)
                            pool.wait_ge(L.summed, p * NG + g + 1)
                            pool.sem_inc(L.allowed, 1)
                            for k in range(GT):
                                pool.indirect_dma_start(
                                    out=rows[:, s, k, 0:width], out_offset=None, in_=table,
                                    in_offset=bass.IndirectOffsetOnAxis(ap=idx_slot[s][:, k:k + 1], axis=0),
                                ).then_inc(L.gathered[s], 16)

            for f in range(4):
                pool.wait_ge(s_t0[f], 16 * len(range(f, NT, 4)))
            gather(L0, table0, ROW0)

            def join(T, u):
                pool.wait_ge(s_parts, T + 1)
                pool.tensor_tensor(yb[:, u, 0, :], yb[:, u, 0, :], yb[:, u, 1, :], ALU.add).then_inc(s_half, 1)
                pool.wait_ge(s_half, T + 1)
                pool.tensor_tensor(yb[:, u, 3, :], yb[:, u, 0, :], yb[:, u, 2, :], ALU.add).then_inc(s_joined, 1)

            def middle(T, u, before, f, before4):
                if not known(T, lambda t: t == NT - 1):
                    join(T + 1, 1 - u)

            join(0, 0)
            over_tiles(pool, middle)

            pool.wait_ge(s_acc, NT)
            pool.memset(sums[:, 0:KD, :], 0.0).then_inc(s_rezero, 1)
            pool.wait_ge(s_t1[0], 16 * ((NT + 1) // 2))
            pool.wait_ge(s_t1[1], 16 * (NT // 2))
            gather(L1, table1, D)

        @block.scalar
        def _(act):
            def first_copy_in(T, u):
                if known(T, lambda t: t == X0):
                    act.wait_ge(s_x[1], 16)
                    act.wait_ge(s_x[2], 16)
                free_of(act, s_xt, T)
                nc.scalar.copy(xs[:, u, :], x_sb[:, bass.ds(T, 1), :].rearrange("p t f -> p (t f)")
                               ).then_inc(s_xs, 1)

            def first_transposed(T, u):
                act.wait_ge(s_xt, T + 1)
                free_of(act, s_tab_ps, T)
                free_of(act, s_xT, T)
                nc.scalar.copy(xTs[:, u, :, :].rearrange("p c n -> p (c n)"), ps[6 + u][:, 0:D]).then_inc(s_xTs, 1)

            def first(T, u, before, f, before4):
                if not known(T, lambda t: t + 1 >= NT):
                    first_transposed(T + 1, 1 - u)
                if not known(T, lambda t: t + 3 >= NT):
                    first_copy_in(T + 3, 1 - u)

            act.wait_ge(s_pads, 3)
            for k, e in enumerate((dst, src, etype)):
                whole = (RC - 1) * RP * P
                act.dma_start(edge_rows[:, k, 0:RC - 1, :],
                              e[0:whole].rearrange("(c r i) -> r c i", c=RC - 1, i=P)).then_inc(s_edges, 16)
                more = EFULL - (RC - 1) * RP
                act.dma_start(edge_rows[0:more, k, RC - 1, :],
                              e[whole:EFULL * P].rearrange("(r i) -> r i", i=P)).then_inc(s_edges, 16)
                act.dma_start(edge_rows[more:more + 1, k, RC - 1, 0:EREM],
                              e[EFULL * P:E].rearrange("(r i) -> r i", r=1)).then_inc(s_edges, 16)
            act.wait_ge(s_x[0], 16)
            first_copy_in(0, 0)
            first_copy_in(1, 1)
            first_transposed(0, 0)
            first_copy_in(2, 0)
            over_tiles(act, first)

            def stage(L, s, g):
                nc.scalar.copy(idx_slot[s][:], idx_tab[:, bass.ds(g * GT, GT)])
                nc.scalar.copy(tab_slot[:, s, :, :], tabs[:, :, bass.ds(g * GT, GT)]).then_inc(L.staged, 1)

            def stage_first(L, p):
                act.wait_ge(L.base, p + 1)
                for g in range(LOOK):
                    stage(L, g, g)

            act.wait_ge(s_passes, 1)
            n_pass = act.value_load(passes_i[0:1, 0:1], min_val=1, max_val=MAXPASS)
            stage_first(L0, 0)
            act.wait_ge(s_dscore, 1)
            for c in range(4):
                nc.scalar.copy(dst_score[:, c * SC:(c + 1) * SC], ps[c][:, :])
            act.drain()
            act.sem_inc(s_dscore_sb, 1)

            with act.Fori(0, n_pass) as p:
                with act.Fori(0, ITERS) as it:
                    for s in range(SLOTS):
                        g = it * SLOTS + s
                        act.wait_ge(L0.score, p * NG + g + 1)
                        nc.scalar.activation(sc[:, s % 2, 2, :], sc[:, s % 2, 1, :], ACT.Exp).then_inc(L0.alpha, 1)
                        act.wait_ge(L0.summed, p * NG + g + SLOTS - 1)
                        stage(L0, (s + LOOK) % SLOTS, g + LOOK)
                        act.wait_ge(L0.staged, p * STAGES + g + 1)
                        for k in range(GT):
                            nc.scalar.activation(hot_rel[:, s % 2, k, 0:R], iota[:, 0:R], ACT.Abs,
                                                 bias=tab_slot[:, s, 2, k:k + 1])
                        act.drain()
                        nc.scalar.activation(hot_rel[:, s % 2, :, 0:R], hot_rel[:, s % 2, :, 0:R], ACT.Relu,
                                             bias=ones[:, 0:1], scale=-1.0).then_inc(L0.hot_rel, 1)
                        act.wait_ge(L0.hot_dst, p * NG + g + 1)
                        nc.scalar.copy(hot_dst_b[:, s % 2, :, :], hot_dst[:, s % 2, :, :]).then_inc(L0.hot_dst_b, 1)
                stage_first(L0, p + 1)

            def copy_sums(T, u):
                free_of(act, s_agg, T)
                nc.scalar.copy(xTs[:, u, :, :], xT[:, :, tile_cols(T)])
                nc.scalar.copy(acc_s[:, u, :, :], sums[:, :, tile_cols(T)]).then_inc(s_acc, 1)

            def parts(T, u):
                act.wait_ge(s_mask, T + 1)
                nc.scalar.activation(yb[:, u, 0, :], ps[2 + u][:, 0:D], ACT.Identity, scale=col[:, u, 0:1])
                nc.scalar.activation(yb[:, u, 1, :], ps[2 + u][:, D:2 * D], ACT.Identity, scale=col[:, u, 1:2])
                nc.scalar.activation(yb[:, u, 2, :], ps[0 + u][:, 0:D], ACT.Relu).then_inc(s_parts, 1)

            def deviation(T, u):
                act.wait_ge(s_var, T + 1)
                nc.scalar.activation(col[:, u, 3:4], mv[:, u, 1:2], ACT.Sqrt, bias=eps_t[:]).then_inc(s_std, 1)

            def middle(T, u, before, f, before4):
                act.wait_ge(s_rstd, T + 1)
                nc.scalar.activation(x1s[:, u, :], yb[:, u, 3, :], ACT.Identity, bias=col[:, u, 5:6],
                                     scale=col[:, u, 4:5]).then_inc(s_x1, 1)
                act.wait_ge(s_x1t, T + 1)
                free_of(act, s_l1, T)
                nc.scalar.copy(x1Ts[:, u, :], ps[4 + u][:, 0:D]).then_inc(s_x1T, 1)
                if not known(T, lambda t: t + 1 >= NT):
                    parts(T + 1, 1 - u)
                act.wait_ge(s_l1, T + 1)
                free_of(act, s_sparse, T)
                nc.scalar.copy(hn[:, u, :], ps[6 + u][:, D:2 * D]).then_inc(s_hn, 1)
                nc.scalar.copy(x_sb[:, bass.ds(T, 1), :].rearrange("p t f -> p (t f)"), ps[6 + u][:, 0:D]
                               ).then_inc(s_res, 1)
                if not known(T, lambda t: t + 1 >= NT):
                    deviation(T + 1, 1 - u)
                if not known(T, lambda t: t + 4 >= NT):
                    copy_sums(T + 4, u)

            act.wait_ge(L0.added, n_pass * (NG + 1) + 1)
            copy_sums(0, 0)
            copy_sums(1, 1)
            parts(0, 0)
            copy_sums(2, 0)
            copy_sums(3, 1)
            deviation(0, 0)
            over_tiles(act, middle)

            stage_first(L1, 0)
            with act.Fori(0, n_pass) as p:
                with act.Fori(0, ITERS) as it:
                    for s in range(SLOTS):
                        g = it * SLOTS + s
                        act.wait_ge(L1.summed, p * NG + g + SLOTS - 1)
                        stage(L1, (s + LOOK) % SLOTS, g + LOOK)
                stage_first(L1, p + 1)

            def copy_last(T, u):
                free_of(act, s_fagg, T)
                nc.scalar.copy(acc_s[:, u, 0:KD, :], sums[:, 0:KD, tile_cols(T)]).then_inc(s_facc, 1)

            def last(T, u, before, f, before4):
                act.wait_ge(s_fvar, T + 1)
                nc.scalar.activation(col[:, u, 3:4], mv[:, u, 1:2], ACT.Sqrt, bias=eps_t[:]).then_inc(s_fstd, 1)
                if not known(T, lambda t: t + 2 >= NT):
                    copy_last(T + 2, u)
                act.wait_ge(s_frstd, T + 1)
                if not known(T, lambda t: t < 4):
                    act.wait_ge(s_out[f], 16 * before4)
                nc.scalar.activation(outs[:, f, :], yb[:, u, 2, :], ACT.Identity, bias=col[:, u, 5:6],
                                     scale=col[:, u, 4:5]).then_inc(s_fout, 1)

            act.wait_ge(L1.added, n_pass * (NG + 1) + 1)
            copy_last(0, 0)
            copy_last(1, 1)
            over_tiles(act, last)

        @block.tensor
        def _(pe):
            pe.sem_inc(L0.summed, SLOTS)
            pe.sem_inc(L1.summed, SLOTS)

            def transpose_edges():
                pe.wait_ge(s_edge_f, 1)
                for k in range(3):
                    for c in range(RC):
                        last = nc.tensor.transpose(ps[3 + k][:, c * RP:(c + 1) * RP], edge_f[:, k, c, :],
                                                   ident[0:RP, 0:RP])
                last.then_inc(s_edge_t, 1)

            def transpose_x(T, u):
                pe.wait_ge(s_xs, T + 1)
                free_of(pe, s_xTs, T)
                for c in range(KD):
                    last = nc.tensor.transpose(ps[6 + u][:, c * P:(c + 1) * P], xs[:, u, c * P:(c + 1) * P], ident[:])
                last.then_inc(s_xt, 1)

            def first(T, u, before, f, before4):
                if not known(T, lambda t: t + 2 >= NT):
                    transpose_x(T + 2, u)
                pe.wait_ge(s_xTs, T + 1)
                free_of(pe, s_tab_sb, T)
                for c in range(KD):
                    last = nc.tensor.matmul(ps[0 + u][:, 0:D + 1], xTs[:, u, c, :], w_tab[:, c, :],
                                            start=(c == 0), stop=(c == KD - 1))
                last.then_inc(s_tab_ps, 1)
                if known(T, lambda t: t == 2):
                    transpose_edges()

            pe.wait_ge(s_ident, 2)
            transpose_x(0, 0)
            transpose_x(1, 1)
            pe.wait_ge(s_wn, 16)
            pe.wait_ge(s_wsrc, 1)
            over_tiles(pe, first)

            pe.wait_ge(s_wvec, 1)
            pe.wait_ge(s_xT, NT)
            pe.wait_ge(s_tab_sb, NT)
            pe.wait_ge(s_span, 1)
            for b in range(4):
                for c in range(KD):
                    last = nc.tensor.matmul(ps[b][:, :], wd_bc[:, c, :], xT[:, c, b * SC:(b + 1) * SC],
                                            start=(c == 0), stop=(c == KD - 1))
            last.then_inc(s_dscore, 1)
            for b in range(4, 7):
                n = min(NPAD, (b + 1) * SC) - b * SC
                for c in range(KD):
                    last = nc.tensor.matmul(ps[b][:, 0:n], wd_bc[:, c, :], xT[:, c, b * SC:b * SC + n],
                                            start=(c == 0), stop=(c == KD - 1))
            last.then_inc(s_dscore, 1)
            pe.wait_ge(s_rel, 32)
            for r in range(2):
                for c in range(KD):
                    last = nc.tensor.transpose(ps[7][:, (2 * c + r) * P:(2 * c + r + 1) * P],
                                               rel_sb[:, r, c * P:(c + 1) * P], ident[:])
            last.then_inc(s_relT, 1)
            pe.wait_ge(s_relT_sb, 1)
            pe.wait_ge(s_dscore_sb, 1)
            for c in range(KD):
                last = nc.tensor.matmul(ps[7][:, 0:R], wr_bc[:, c, :], relT[:, c, 0:R],
                                        start=(c == 0), stop=(c == KD - 1))
            last.then_inc(s_relp, 1)
            for r in range(2):
                for c in range(KD):
                    last = nc.tensor.matmul(ps[3][:, r * D:(r + 1) * D], relT[:, c, r * P:(r + 1) * P],
                                            w_tab[:, c, 0:D], start=(c == 0), stop=(c == KD - 1))
            last.then_inc(s_relp, 1)

            pe.wait_ge(s_setup, 1)
            pe.wait_ge(s_passes, 1)
            n_pass = pe.value_load(passes_i[0:1, 0:1], min_val=1, max_val=MAXPASS)
            with pe.Fori(0, n_pass) as p:
                with pe.Fori(0, ITERS) as it:
                    for s in range(SLOTS):
                        g = it * SLOTS + s
                        pe.wait_ge(L0.added, p * (NG + 1) + g + 1)
                        pe.wait_ge(L0.hot_dst, p * NG + g + 1)
                        for q in range(KD):
                            for k in range(GT):
                                nc.tensor.matmul(ps[s % 2][:, q * P:(q + 1) * P], rows[:, s, k, q * P:(q + 1) * P],
                                                 hot_dst[:, s % 2, k, :], start=(k == 0), stop=(k == GT - 1))
                        pe.wait_ge(L0.hot_rel, p * NG + g + 1)
                        pe.wait_ge(L0.hot_dst_b, p * NG + g + 1)
                        for r in range(2):
                            for k in range(GT):
                                last = nc.tensor.matmul(ps[s % 2][:, (KD + r) * P:(KD + r + 1) * P],
                                                        hot_rel[:, s % 2, k, r * P:(r + 1) * P],
                                                        hot_dst_b[:, s % 2, k, :], start=(k == 0), stop=(k == GT - 1))
                        last.then_inc(L0.summed, 1)

            def node_products(T, u):
                pe.wait_ge(s_acc, T + 1)
                if not known(T, lambda t: t < 2):
                    pe.wait_ge(s_parts, T - 1)
                for r in range(2):
                    nc.tensor.matmul(ps[0 + u][:, 0:D + 1], acc_s[:, u, KD + r, :], rel_tab[:, r, :],
                                     start=(r == 0), stop=False)
                for c in range(KD):
                    nc.tensor.matmul(ps[0 + u][:, c * P:(c + 1) * P], acc_s[:, u, c, :], ident[:],
                                     start=False, stop=(c == KD - 1))
                for c in range(KD):
                    last = nc.tensor.matmul(ps[2 + u][:, :], xTs[:, u, c, :], w_loops[:, c, :],
                                            start=(c == 0), stop=(c == KD - 1))
                last.then_inc(s_agg, 1)

            def middle(T, u, before, f, before4):
                pe.wait_ge(s_x1, T + 1)
                free_of(pe, s_x1T, T)
                for c in range(KD):
                    last = nc.tensor.transpose(ps[4 + u][:, c * P:(c + 1) * P], x1s[:, u, c * P:(c + 1) * P], ident[:])
                last.then_inc(s_x1t, 1)
                pe.wait_ge(s_x1T, T + 1)
                free_of(pe, s_res, T)
                for c in range(KD):
                    last = nc.tensor.matmul(ps[6 + u][:, :], x1Ts[:, u, c * P:(c + 1) * P], w_l1[:, c, :],
                                            start=(c == 0), stop=(c == KD - 1))
                last.then_inc(s_l1, 1)
                if not known(T, lambda t: t + 3 >= NT):
                    node_products(T + 3, 1 - u)

            pe.wait_ge(s_w_plus, 1)
            node_products(0, 0)
            node_products(1, 1)
            node_products(2, 0)
            over_tiles(pe, middle)

            pe.wait_ge(s_parts, NT)
            with pe.Fori(0, n_pass) as p:
                with pe.Fori(0, ITERS) as it:
                    for s in range(SLOTS):
                        g = it * SLOTS + s
                        pe.wait_ge(L1.added, p * (NG + 1) + g + 1)
                        pe.wait_ge(L1.hot_dst, p * NG + g + 1)
                        pe.wait_ge(L1.gathered[s], (p * ITERS + it + 1) * GT * 16)
                        for q in range(KD):
                            for k in range(GT):
                                last = nc.tensor.matmul(ps[s % 2][:, q * P:(q + 1) * P],
                                                        rows[:, s, k, q * P:(q + 1) * P], hot_dst[:, s % 2, k, :],
                                                        start=(k == 0), stop=(k == GT - 1))
                        last.then_inc(L1.summed, 1)

            def last_rows(T, u, before, f, before4):
                pe.wait_ge(s_facc, T + 1)
                free_of(pe, s_fvar, T)
                for c in range(KD):
                    last = nc.tensor.transpose(ps[2 + u][:, c * P:(c + 1) * P], acc_s[:, u, c, :], ident[:])
                last.then_inc(s_fagg, 1)
            over_tiles(pe, last_rows)

        @block.vector
        def _(dve):
            V = nc.vector

            def settle():
                dve.drain()

            V.memset(ones[:], 1.0)
            V.memset(tab_out[:], 0.0)

            dve.wait_ge(s_wa, 32)
            for c in range(KD):
                V.tensor_tensor_reduce(out=w3_first[:, c, :], in0=w3_first[:, c, :], in1=a_bc, scale=1.0, scalar=0.0,
                                       op0=ALU.mult, op1=ALU.add, accum_out=w_vec[:, c:c + 1])
            settle()
            V.tensor_copy(w_tab[:, :, D:D + 1].rearrange("p c o -> p (c o)"), w_vec[:, 0:KD]).then_inc(s_wsrc, 1)
            V.memset(eps_t[:], EPS)
            V.memset(tabs[:], 0.0)
            V.memset(idx_tab[:], 0)
            V.memset(base_i[:], 0)
            dve.wait_ge(s_ones, 1)
            V.tensor_copy(iota[:], iota_i)

            def edge_floats():
                dve.wait_ge(s_edges, 9 * 16)
                V.tensor_copy(edge_f[:, :, :, :].rearrange("r k c i -> r k (c i)"),
                              edge_rows[:, :, :, :].rearrange("r k c i -> r k (c i)")).then_inc(s_edge_f, 1)

            def edge_tables():
                dve.wait_ge(s_edge_t, 1)
                V.tensor_copy(dst_f[:], ps[3][:, 0:NE])
                V.tensor_copy(idx_tab[:, 0:NE], ps[4][:, 0:NE])
                V.tensor_copy(tabs[:, 1, 0:NE], ps[5][:, 0:NE])
                settle()
                V.tensor_scalar(tabs[:, 2, 0:NE], tabs[:, 1, 0:NE], -1.0, None, ALU.mult)
                V.memset(hot_rel[:, :, :, R:256], 0.0)
                V.tensor_reduce(span_in[:, 1, :], dst_f[:].rearrange("p (g k) -> p g k", k=GT), AX.X, ALU.max)
                V.tensor_reduce(base_cur[:], dst_f[:].rearrange("p (g k) -> p g k", k=GT), AX.X, ALU.min)
                settle()
                V.tensor_scalar(span_in[:, 0, :], base_cur[:], -1.0, None, ALU.mult).then_inc(s_span, 1)

            def count_passes():
                dve.wait_ge(s_spanned, 1)
                V.tensor_tensor(base_cur[:], span[:, 0, :], span[:, 1, :], ALU.add)
                settle()
                V.reduce_max(flags[:, 0:1], base_cur[:], AX.X)
                settle()
                V.tensor_scalar(flags[:, 1:2], flags[:, 0:1], float(P), None, ALU.is_ge)
                V.tensor_scalar(flags[:, 2:3], flags[:, 0:1], float(P), None, ALU.is_lt)
                settle()
                V.tensor_scalar(passes_i[:], flags[:, 1:2], float(MAXPASS - 1), 1.0, ALU.mult, ALU.add)
                V.tensor_scalar(base0[:], span[:, 0, :], flags[:, 2:3], -1.0, ALU.mult, ALU.mult)
                settle()
                V.sem_inc(s_passes, 1)

            def set_windows(L):
                V.tensor_copy(base_i[:, 1:1 + NG], base_cur[:])
                V.tensor_tensor(tabs[:, 0, 0:NE].rearrange("p (g k) -> p g k", k=GT),
                                dst_f[:].rearrange("p (g k) -> p g k", k=GT),
                                base_cur[:].unsqueeze(2).broadcast_to([P, NG, GT]), ALU.subtract)
                settle()
                dve.sem_inc(L.base, 1)

            def begin_layer(L):
                V.tensor_copy(base_cur[:], base0[:])
                settle()
                set_windows(L)

            def first(T, u, before, f, before4):
                dve.wait_ge(s_xTs, T + 1)
                V.tensor_copy(xT[:, :, tile_cols(T)], xTs[:, u, :, :]).then_inc(s_xT, 1)
                dve.wait_ge(s_tab_ps, T + 1)
                if not known(T, lambda t: t < 4):
                    dve.wait_ge(s_t0[f], before4 * 16)
                V.tensor_copy(tab_out[:, f, 0:D + 1], ps[0 + u][:, 0:D + 1]).then_inc(s_tab_sb, 1)
                if known(T, lambda t: t == 1):
                    edge_floats()
                if known(T, lambda t: t == 2):
                    edge_tables()
                if known(T, lambda t: t == 3):
                    count_passes()
                    begin_layer(L0)
            over_tiles(dve, first)

            dve.wait_ge(s_w3a, 1)
            V.tensor_reduce(w_vec[:, KD:6], w3_rest, AX.X, ALU.add)
            settle()
            for c in range(KD):
                V.tensor_scalar(wd_bc[:, c, :], ones[:], w_vec[:, 2 + c:3 + c], None, ALU.mult)
                last = V.tensor_scalar(wr_bc[:, c, :], ones[:], w_vec[:, 4 + c:5 + c], None, ALU.mult)
            last.then_inc(s_wvec, 1)
            dve.wait_ge(s_dscore, 2)
            for b in range(4, 7):
                n = min(NPAD, (b + 1) * SC) - b * SC
                V.tensor_copy(dst_score[:, b * SC:b * SC + n], ps[b][:, 0:n])
            dve.wait_ge(s_relT, 1)
            V.tensor_copy(relT.rearrange("p c r -> p (c r)"), ps[7][:, :]).then_inc(s_relT_sb, 1)
            dve.wait_ge(s_relp, 2)
            V.tensor_copy(rel_score[:], ps[7][:, 0:R])
            V.tensor_copy(rel_tab[:, :, 0:D], ps[3][:, :].rearrange("p (r f) -> p r f", r=2))
            V.memset(rel_tab[:, :, D:D + 1], 1.0).then_inc(s_setup, 1)
            dve.wait_ge(s_dscore_sb, 1)
            for f in range(4):
                dve.wait_ge(s_t0[f], 16 * len(range(f, NT, 4)))

            dve.wait_ge(s_zero, 2)
            dve.sem_inc(L0.added, 1)
            dve.sem_inc(L1.added, 1)
            n_pass = dve.value_load(passes_i[0:1, 0:1], min_val=1, max_val=MAXPASS)

            def add_window(L, p, g, s, width):
                base = dve.value_load(base_i[0:1, bass.ds(g, 1)], min_val=0, max_val=N)
                dve.wait_ge(L.added, p * (NG + 1) + g + 1)
                dve.wait_ge(L.summed, p * NG + g + SLOTS)
                win = sums[:, 0:width, bass.ds(base, P)]
                V.tensor_tensor(win, win, ps[(s + 1) % 2][:, 0:width * P].rearrange("p (q n) -> p q n", n=P),
                                ALU.add).then_inc(L.added, 1)

            def end_pass(L, p):
                dve.wait_ge(L.staged, (p + 1) * STAGES)
                V.tensor_scalar(base_cur[:], base_cur[:], float(P), None, ALU.add)
                settle()
                set_windows(L)

            def window_base(g):
                return dve.value_load(base_i[0:1, bass.ds(g + 1, 1)], min_val=0, max_val=N)

            def look_up(base, b, s, k, which):
                if which == "dst":
                    return V.scalar_tensor_tensor(out=products_d[:, k, :], in0=iota[:, 0:P],
                                                  scalar=tab_slot[:, s, 0, k:k + 1],
                                                  in1=dst_score[:, bass.ds(base, P)], op0=ALU.is_equal,
                                                  op1=ALU.mult, accum_out=score_dst[:, b, k:k + 1])
                return V.scalar_tensor_tensor(out=products_r[:, k, :], in0=iota[:, 0:R],
                                              scalar=tab_slot[:, s, 1, k:k + 1], in1=rel_score[:],
                                              op0=ALU.is_equal, op1=ALU.mult, accum_out=score_rel[:, b, k:k + 1])

            with dve.Fori(0, n_pass) as p:
                V.memset(ps[1][:, :], 0.0)
                settle()
                base = window_base(0)
                dve.wait_ge(L0.staged, p * STAGES + 1)
                for which in ("dst", "rel"):
                    for k in range(GT):
                        last = look_up(base, 0, 0, k, which)
                last.then_inc(L0.looked_up, 1)
                with dve.Fori(0, ITERS) as it:
                    for s in range(SLOTS):
                        g = it * SLOTS + s
                        b, b1, s1 = s % 2, (s + 1) % 2, (s + 1) % SLOTS
                        base = window_base(g + 1)
                        nth = dve.snap(p * NG + g + 1)
                        looked = dve.snap(p * (NG + 1) + g + 1)
                        dve.wait_ge(L0.staged, p * STAGES + g + 2)
                        dve.wait_ge(L0.looked_up, looked)
                        look_up(base, b1, s1, 0, "dst")
                        V.tensor_tensor(sc[:, b, 0, :], score_dst[:, b, :], score_rel[:, b, :],
                                        ALU.add).then_inc(L0.joined, 1)
                        for k in (1, 2):
                            look_up(base, b1, s1, k, "dst")
                        dve.wait_ge(L0.gathered[s], (p * ITERS + it + 1) * GT * 16)
                        dve.wait_ge(L0.joined, nth)
                        V.tensor_tensor(sc[:, b, 0, :], sc[:, b, 0, :], rows[:, s, :, D], ALU.add).then_inc(L0.scored, 1)
                        for k in (3, 4):
                            look_up(base, b1, s1, k, "dst")
                        dve.wait_ge(L0.scored, nth)
                        V.scalar_tensor_tensor(out=sc[:, b, 1, :], in0=sc[:, b, 0, :], scalar=0.01,
                                               in1=sc[:, b, 0, :], op0=ALU.mult, op1=ALU.max).then_inc(L0.score, 1)
                        for k in (5, 6, 7):
                            look_up(base, b1, s1, k, "dst")
                        look_up(base, b1, s1, 0, "rel")
                        dve.wait_ge(L0.alpha, nth)
                        V.tensor_scalar(sc[:, b, 3, :], sc[:, b, 2, :], 0.25, None, ALU.mult).then_inc(L0.quarter, 1)
                        for k in (1, 2):
                            look_up(base, b1, s1, k, "rel")
                        dve.wait_ge(L0.quarter, nth)
                        V.reciprocal(sc[:, b, 4, :], sc[:, b, 3, :]).then_inc(L0.inverse, 1)
                        for k in (3, 4):
                            look_up(base, b1, s1, k, "rel")
                        dve.wait_ge(L0.inverse, nth)
                        V.tensor_tensor(sc[:, b, 5, :], sc[:, b, 3, :], sc[:, b, 4, :], ALU.mult).then_inc(L0.weight, 1)
                        for k in (5, 6):
                            look_up(base, b1, s1, k, "rel")
                        look_up(base, b1, s1, 7, "rel").then_inc(L0.looked_up, 1)
                        dve.wait_ge(L0.summed, p * NG + g + SLOTS - 1)
                        dve.wait_ge(L0.weight, nth)
                        for k in range(GT):
                            last = V.tensor_scalar(hot_dst[:, b, k, :], iota[:, 0:P], tab_slot[:, s, 0, k:k + 1],
                                                   sc[:, b, 5, k:k + 1], ALU.is_equal, ALU.mult)
                        last.then_inc(L0.hot_dst, 1)
                        add_window(L0, p, g, s, 4)
                add_window(L0, p, NG, NG, 4)
                end_pass(L0, p)

            def write_sparse(T, u, before):
                dve.wait_ge(s_top, T + 1)
                if not known(T, lambda t: t < 2):
                    dve.wait_ge(s_t1[u], before * 16)
                V.scalar_tensor_tensor(out=sparse[:, u, :], in0=work[:, u, :], scalar=LOWEST, in1=hn[:, u, :],
                                       op0=ALU.is_equal, op1=ALU.mult).then_inc(s_sparse, 1)

            def node_step(T, u, join=True, top=True):
                last_one = known(T, lambda t: t == NT)
                v = 1 - u
                if not last_one:
                    dve.wait_ge(s_std, T + 1)
                if join:
                    dve.wait_ge(s_agg, T + 2)
                if top:
                    dve.wait_ge(s_hn, T)

                def top_half(r, half):
                    source = hn[:, v, :] if r == 0 else work[:, v, :]
                    if top and half == 0:
                        V.max(top8[:, v, :], source)
                    elif top:
                        return V.match_replace(work[:, v, :], top8[:, v, :], source, LOWEST)

                if not last_one:
                    V.reciprocal(col[:, u, 4:5], col[:, u, 3:4])
                if join:
                    count = ps[0 + v][:, D:D + 1]
                    V.tensor_scalar(col[:, v, 0:1], count, 0.0, None, ALU.is_gt)
                    V.tensor_scalar(col[:, v, 1:2], count, 0.0, None, ALU.is_le)
                    V.tensor_scalar(col[:, v, 2:3], count, 1.0, None, ALU.max)
                top_half(0, 0)
                settle()
                if not last_one:
                    V.tensor_scalar(col[:, u, 5:6], mv[:, u, 0:1], col[:, u, 4:5], -1.0, ALU.mult,
                                    ALU.mult).then_inc(s_rstd, 1)
                if join:
                    V.reciprocal(r_deg[:, bass.ds(T + 1, 1)], col[:, v, 2:3]).then_inc(s_mask, 1)
                top_half(0, 1)
                for r in range(1, TOPK // 8):
                    if top:
                        settle()
                    top_half(r, 0)
                    if join and r == TOPK // 8 - 1:
                        dve.wait_ge(s_joined, T + 2)
                        V.bn_stats(bn[:, v, :], yb[:, v, 3, :])
                    if top or join:
                        settle()
                    last = top_half(r, 1)
                if top:
                    last.then_inc(s_top, 1)
                if join:
                    V.bn_aggr(mv[:, v, :], bn[:, v, :]).then_inc(s_var, 1)

            dve.wait_ge(s_agg, 1)
            V.tensor_scalar(col[:, 0, 0:1], ps[0][:, D:D + 1], 0.0, None, ALU.is_gt)
            V.tensor_scalar(col[:, 0, 1:2], ps[0][:, D:D + 1], 0.0, None, ALU.is_le)
            V.tensor_scalar(col[:, 0, 2:3], ps[0][:, D:D + 1], 1.0, None, ALU.max)
            settle()
            V.reciprocal(r_deg[:, 0:1], col[:, 0, 2:3]).then_inc(s_mask, 1)
            dve.wait_ge(s_joined, 1)
            V.bn_stats(bn[:, 0, :], yb[:, 0, 3, :])
            settle()
            V.bn_aggr(mv[:, 0, :], bn[:, 0, :]).then_inc(s_var, 1)

            def middle(T, u, before, f, before4):
                if not known(T, lambda t: t < 2):
                    write_sparse(T - 2, u, before - 1)
                node_step(T, u, join=not known(T, lambda t: t == NT - 1), top=not known(T, lambda t: t == 0))
            over_tiles(dve, middle)
            write_sparse(NT - 2, 1, NT // 2 - 1)
            node_step(NT, 1, join=False)
            write_sparse(NT - 1, 0, NT // 2)

            begin_layer(L1)
            dve.wait_ge(s_rezero, 1)
            with dve.Fori(0, n_pass) as p:
                V.memset(ps[1][:, :], 0.0)
                settle()
                with dve.Fori(0, ITERS) as it:
                    for s in range(SLOTS):
                        g = it * SLOTS + s
                        dve.wait_ge(L1.staged, p * STAGES + g + 1)
                        dve.wait_ge(L1.summed, p * NG + g + SLOTS - 1)
                        V.tensor_tensor(hot_dst[:, s % 2, :, :], iota[:, 0:P].unsqueeze(1).broadcast_to([P, GT, P]),
                                        tab_slot[:, s, 0, :].unsqueeze(2).broadcast_to([P, GT, P]),
                                        ALU.is_equal).then_inc(L1.hot_dst, 1)
                        add_window(L1, p, g, s, KD)
                add_window(L1, p, NG, NG, KD)
                end_pass(L1, p)

            def scale_of(T, u):
                V.tensor_scalar(col[:, u, 5:6], mv[:, u, 0:1], col[:, u, 4:5], -1.0, ALU.mult,
                                ALU.mult).then_inc(s_frstd, 1)

            def last(T, u, before, f, before4):
                dve.wait_ge(s_fagg, T + 1)
                free_of(dve, s_fout, T)
                V.scalar_tensor_tensor(out=yb[:, u, 2, :], in0=ps[2 + u][:, 0:D], scalar=r_deg[:, bass.ds(T, 1)],
                                       in1=x_sb[:, bass.ds(T, 1), :].rearrange("p t f -> p (t f)"),
                                       op0=ALU.mult, op1=ALU.add)
                if not known(T, lambda t: t == 0):
                    dve.wait_ge(s_fstd, T)
                    V.reciprocal(col[:, 1 - u, 4:5], col[:, 1 - u, 3:4])
                settle()
                V.bn_stats(bn[:, u, :], yb[:, u, 2, :])
                if not known(T, lambda t: t == 0):
                    scale_of(T - 1, 1 - u)
                settle()
                V.bn_aggr(mv[:, u, :], bn[:, u, :]).then_inc(s_fvar, 1)
            over_tiles(dve, last)
            dve.wait_ge(s_fstd, NT)
            V.reciprocal(col[:, 0, 4:5], col[:, 0, 3:4])
            settle()
            scale_of(NT - 1, 0)


_INS = ["x", "src", "dst", "edge_type_200", "L0_gnn_rel_emb", "L0_gnn_weight_neighbor", "L0_gnn_a", "L0_gnn_W3",
        "L0_gnn_loop_weight", "L0_gnn_evolve_loop_weight", "L1_gnn_W_self", "L1_gnn_W_neigh"]


def kernel(**inputs):
    import numpy as _np
    import concourse.bacc as _bacc
    from concourse import mybir as _mybir
    from concourse.bass_utils import run_bass_kernel_spmd as _run

    nc = _bacc.Bacc("TRN2", target_bir_lowering=False, num_devices=1)
    arrays, args = {}, []
    for name in _INS:
        arr = _np.ascontiguousarray(inputs[name])
        arrays[f"in_{name}_dram"] = arr
        args.append(nc.dram_tensor(f"in_{name}_dram", arr.shape, _mybir.dt.from_np(arr.dtype),
                                   kind="ExternalInput").ap())
    args.append(nc.dram_tensor("out_0_dram", tuple(inputs["x"].shape), _mybir.dt.float32,
                               kind="ExternalOutput").ap())
    gnn_two_layers(nc, *args)
    r = _run(nc, [arrays], core_ids=[0])
    return r.results[0]["out_0_dram"]
```

```python
from contextlib import ExitStack

import concourse.bass as bass
from concourse import mybir



def gnn_two_layers(nc, x, src, dst, etype, rel_emb, w_neighbor, a, w3, loop_w, evolve_w, w_self, w_neigh, out):
    f32, i32, bf16 = mybir.dt.float32, mybir.dt.int32, mybir.dt.bfloat16
    ALU, ACT, AX = mybir.AluOpType, mybir.ActivationFunctionType, mybir.AxisListType
    RMAX = bass.bass_isa.ReduceOp.max

    P = 128
    N, D = x.shape
    E = src.shape[0]
    R = rel_emb.shape[0]
    KD = D // P
    NT = -(-N // P)
    TAIL = N - (NT - 1) * P
    NPAD = NT * P
    EFULL = E // P
    EREM = E - EFULL * P
    GT = 8
    SLOTS = 4
    NG = -(-(EFULL + 1) // (GT * SLOTS)) * SLOTS
    ITERS = NG // SLOTS
    NE = NG * GT
    LOOK = 2
    RC = 4
    RP = NE // RC
    STAGES = NG + LOOK
    ROW0 = 272
    NACC = N + P
    TOPK = 32
    EPS = 1e-5
    LOWEST = -3.4028234663852886e38
    MAXPASS = NT
    X0 = 4
    score_bank = (0, 1, 2, 4, 5, 6, 0)
    LT = max(NT, 2 * ITERS)
    SC = 512

    table0 = nc.dram_tensor("table0", (NPAD, ROW0), f32).ap()
    table1 = nc.dram_tensor("table1", (NPAD, D), f32).ap()

    ctx = ExitStack()
    with ctx:
        def sb(name, shape, dt=f32):
            return ctx.enter_context(nc.sbuf_tensor(name, shape, dt))

        def sem(name):
            return ctx.enter_context(nc.semaphore(name))

        ident = sb("ident", [P, P])
        iota = sb("iota", [P, 256])
        ones = sb("ones", [P, P])
        eps_t = sb("eps_t", [P, 1])
        root = sb("root", [P, 1])
        x_sb = sb("x_sb", [P, LT, D])
        xT = sb("xT", [P, KD, LT * P])
        sums = sb("sums", [P, 4, NACC])
        dst_score = sb("dst_score", [P, NACC])
        rel_score = sb("rel_score", [P, R])
        rows = sb("rows", [P, SLOTS, GT, ROW0])
        hot_dst = sb("hot_dst", [P, 2, GT, P])
        hot_dst_b = sb("hot_dst_b", [P, 2, GT, P], bf16)
        hot_rel = sb("hot_rel", [P, 2, GT, 256], bf16)
        w_tab = sb("w_tab", [P, KD, D + 1])
        w_loops = sb("w_loops", [P, KD, 2 * D])
        w_l1 = sb("w_l1", [P, KD, 2 * D])
        w_vec = sb("w_vec", [P, 6])
        wd_bc = sb("wd_bc", [P, KD, P])
        rel_tab = sb("rel_tab", [P, 2, D + 1])
        tabs = sb("tabs", [P, 3, STAGES * GT])
        dst_f = sb("dst_f", [P, NE])
        idx_tab = sb("idx_tab", [P, STAGES * GT], i32)
        tab_slot = sb("tab_slot", [P, SLOTS, 3, GT])
        idx_slot = [sb(f"idx_slot{s}", [P, GT], i32) for s in range(SLOTS)]
        span_in = sb("span_in", [P, 2, NG])
        span = sb("span", [P, 2, NG])
        base0 = sb("base0", [P, NG])
        base_cur = sb("base_cur", [P, NG])
        base_i = sb("base_i", [P, 2 + NG], i32)
        flags = sb("flags", [P, 8])
        passes_i = sb("passes_i", [P, 1], i32)
        score_dst = sb("score_dst", [P, 2, GT])
        score_rel = sb("score_rel", [P, 2, GT])
        sc = sb("sc", [P, 2, 6, GT])
        degree = sb("degree", [P, NT])
        r_deg = sb("r_deg", [P, NT])
        node_slots = sb("node_slots", [P, 4, D])
        xs = node_slots[:, 0:2, :]
        xTs = node_slots[:, 2:4, :].rearrange("p u (c n) -> p u c n", c=KD)
        products_r = node_slots[:].rearrange("p a f -> p (a f)")[:, 0:GT * R // 2].bitcast(bf16).rearrange(
            "p (k r) -> p k r", k=GT)
        tab_out = sb("tab_out", [P, 4, ROW0])
        products_d = tab_out[:].rearrange("p u w -> p (u w)")[:, 0:GT * P // 2].bitcast(bf16).rearrange(
            "p (k n) -> p k n", k=GT)
        loop_xT = tab_out[:].rearrange("p u w -> p (u w)")[:, GT * P // 2:GT * P // 2 + D].rearrange(
            "p (c n) -> p c n", c=KD)
        col = sb("col", [P, 2, 3])
        has_edges = sb("has_edges", [P, 2, 2])
        bn = sb("bn", [P, 2, 6])
        mv = sb("mv", [P, 2, 2])
        a_bc = hot_dst[:, 0, :, :].rearrange("p k n -> p (k n)")[:, 0:3 * D]
        rows_flat = rows[:].rearrange("p s k w -> p (s k w)")
        flat_used = [0]

        def in_rows(*shape):
            n = 1
            for d in shape:
                n *= d
            at = flat_used[0]
            flat_used[0] += n
            assert flat_used[0] <= SLOTS * GT * ROW0
            names = "abcd"[:len(shape)]
            return rows_flat[:, at:at + n].rearrange(f"p ({' '.join(names)}) -> p {' '.join(names)}",
                                                     **dict(zip(names, shape)))

        w3_first = in_rows(KD, 3 * D)
        iota_i = in_rows(256).bitcast(i32)
        flat_used[0] = GT * ROW0
        edge_rows = in_rows(3, RC, P).bitcast(i32)[0:RP]
        flat_used[0] = 2 * GT * ROW0
        w3_rest = in_rows(6 - KD, 3 * D)
        rel_sb = in_rows(2, D)
        relT = in_rows(KD, 256)
        wr_bc = in_rows(KD, P)
        flat_used[0] = 0
        x1Ts = in_rows(2, D)
        acc_s = in_rows(2, 4, P)
        yb = in_rows(2, 4, D)
        x1s = in_rows(2, D)
        hn = in_rows(4, D)
        work = in_rows(4, D)
        sparse = in_rows(4, D)
        outs = in_rows(4, D)
        acc_last = acc_s.rearrange("p u (h c) n -> p (u h) c n", h=2)
        last_rows_sb = yb.rearrange("p u q f -> p (u q) f")
        edge_f = hot_rel[:].rearrange("p s k w -> p (s k w)").bitcast(f32)[0:RP, 0:3 * RC * P].rearrange(
            "p (a c i) -> p a c i", a=3, c=RC)
        top8 = sb("top8", [P, 4, 8])

        ps = [ctx.enter_context(nc.psum_tensor(f"ps{b}", [P, 512], f32)) for b in range(8)]

        s_ident = sem("s_ident")
        s_pads = sem("s_pads")
        s_ones = sem("s_ones")
        s_eps = sem("s_eps")
        s_edges = sem("s_edges")
        s_rel = sem("s_rel")
        s_w3 = sem("s_w3")
        s_wn = sem("s_wn")
        s_x = [sem(f"s_x_load{c}") for c in range(4)]
        s_wa = sem("s_wa")
        s_wsrc = sem("s_wsrc")
        s_w3a = sem("s_w3a")
        s_dscore = sem("s_dscore")
        s_dscore_sb = sem("s_dscore_sb")
        s_w = sem("s_w")
        s_w_plus = sem("s_w_plus")
        s_zero = sem("s_zero")
        s_edge_f = sem("s_edge_f")
        s_edge_t = sem("s_edge_t")
        s_span = sem("s_span")
        s_spanned = sem("s_spanned")
        s_passes = sem("s_passes")
        s_wvec = sem("s_wvec")
        s_relT = sem("s_relT")
        s_relT_sb = sem("s_relT_sb")
        s_relp = sem("s_relp")
        s_setup = sem("s_setup")
        s_xs = sem("s_xs")
        s_xt = sem("s_xt")
        s_xTs = sem("s_xTs")
        s_xT = sem("s_xT")
        s_tab_ps = sem("s_tab_ps")
        s_tab_sb = sem("s_tab_sb")
        s_t0 = [sem(f"s_t0_{f}") for f in range(4)]
        s_acc = sem("s_acc")
        s_loop_in = sem("s_loop_in")
        s_loop_ps = sem("s_loop_ps")
        s_agg = sem("s_agg")
        s_mask = sem("s_mask")
        s_parts = sem("s_parts")
        s_half = sem("s_half")
        s_joined = sem("s_joined")
        s_var = sem("s_var")
        s_std = sem("s_std")
        s_rstd = sem("s_rstd")
        s_x1 = sem("s_x1")
        s_x1t = sem("s_x1t")
        s_x1T = sem("s_x1T")
        s_l1 = sem("s_l1")
        s_hn = sem("s_hn")
        s_res = sem("s_res")
        s_sparse = sem("s_sparse")
        s_t1 = [sem(f"s_t1_{f}") for f in range(4)]
        s_rezero = sem("s_rezero")
        s_facc = sem("s_facc")
        s_fagg = sem("s_fagg")
        s_fvar = sem("s_fvar")
        s_fstd = sem("s_fstd")
        s_frstd = sem("s_frstd")
        s_fout = sem("s_fout")
        s_out = [sem(f"s_out{f}") for f in range(4)]

        class Layer:
            def __init__(self, tag):
                self.base = sem(f"base_ready{tag}")
                self.staged = sem(f"staged{tag}")
                self.allowed = sem(f"allowed{tag}")
                self.gathered = [sem(f"gathered{tag}_{s}") for s in range(SLOTS)]
                self.hot_rel = sem(f"hot_rel{tag}")
                self.score = sem(f"score{tag}")
                self.alpha = sem(f"alpha{tag}")
                self.hot_dst = sem(f"hot_dst{tag}")
                self.hot_dst_b = sem(f"hot_dst_b{tag}")
                self.looked_up = sem(f"looked_up{tag}")
                self.joined = sem(f"joined{tag}")
                self.scored = sem(f"scored{tag}")
                self.quarter = sem(f"quarter{tag}")
                self.inverse = sem(f"inverse{tag}")
                self.weight = sem(f"weight{tag}")
                self.summed = sem(f"summed{tag}")
                self.added = sem(f"added{tag}")

        L0, L1 = Layer("0"), Layer("1")

        def over_tiles(eng, step, head=4):
            loops = (NT - 3 - head) // 4
            for T in range(head):
                step(T, T % 2, T // 2, T % 4, T // 4)
            with eng.Fori(0, loops) as it:
                for h in range(head, head + 4):
                    step(eng.snap(it * 4 + h), h % 2, it * 2 + h // 2, h % 4, it + h // 4)
            for T in range(head + 4 * loops, NT):
                step(T, T % 2, T // 2, T % 4, T // 4)

        def known(T, test):
            return isinstance(T, int) and test(T)

        def free_of(eng, done, T):
            if not known(T, lambda t: t < 2):
                eng.wait_ge(done, T - 1)

        def tile_cols(T):
            return bass.ds(T * P, P)

        block = ctx.enter_context(nc.Block())

        @block.sync
        def _(sp):
            w3_rows = w3.rearrange("(c p) k -> p c k", p=P)
            x_tiles = x[0:(NT - 1) * P, :].rearrange("(t p) f -> p t f", p=P)
            sp.dma_start(w3_first, w3_rows[:, 0:KD, :]).then_inc(s_wa, 16)
            sp.dma_start(a_bc, a.rearrange("k o -> o k").broadcast_to([P, 3 * D])).then_inc(s_wa, 16)
            sp.dma_start(x_sb[:, 0:X0, :], x_tiles[:, 0:X0, :]).then_inc(s_x[0], 16)
            sp.dma_start(w_tab[:, :, 0:D], w_neighbor.rearrange("(c p) f -> p c f", p=P)).then_inc(s_wn, 16)
            sp.dma_start(x_sb[:, X0:2 * X0, :], x_tiles[:, X0:2 * X0, :]).then_inc(s_x[3], 16)
            for t in range(2 * X0, NT - 1, 2):
                sp.dma_start(x_sb[:, t:t + 2, :], x_tiles[:, t:t + 2, :]).then_inc(s_x[1], 16)
            sp.wait_ge(s_pads, 5)
            sp.dma_start(x_sb[0:TAIL, NT - 1, :], x[(NT - 1) * P:N, :]).then_inc(s_x[2], 16)

            def load_more(k):
                if k < 6 - KD:
                    sp.dma_start(w3_rest[:, k, :], w3_rows[:, KD + k, :]).then_inc(s_w3, 16)
                elif k == 6 - KD:
                    sp.dma_start(rel_sb[:, 0, :], rel_emb[0:P, :]).then_inc(s_rel, 16)
                    sp.dma_start(rel_sb[0:R - P, 1, :], rel_emb[P:R, :]).then_inc(s_rel, 16)
                elif k == 7 - KD:
                    sp.dma_start(w_loops[:, :, 0:D], loop_w.rearrange("(c p) f -> p c f", p=P)).then_inc(s_w, 16)
                    sp.dma_start(w_loops[:, :, D:2 * D], evolve_w.rearrange("(c p) f -> p c f", p=P)).then_inc(s_w, 16)
                elif k == 8 - KD:
                    sp.dma_start(w_l1[:, :, 0:D], w_self.rearrange("(c p) f -> p c f", p=P)).then_inc(s_w, 16)
                    sp.dma_start(w_l1[:, :, D:2 * D], w_neigh.rearrange("(c p) f -> p c f", p=P)).then_inc(s_w, 16)

            def store_table0(T, u, before, f, before4):
                sp.wait_ge(s_tab_sb, T + 1)
                sp.dma_start(table0[tile_cols(T), :], tab_out[:, f, :]).then_inc(s_t0[f], 16)
                if isinstance(T, int):
                    load_more(T)
            over_tiles(sp, store_table0, head=2 * X0)

            def store_table1(T, u, before, f, before4):
                sp.wait_ge(s_sparse, T + 1)
                sp.dma_start(table1[tile_cols(T), :], sparse[:, f, :]).then_inc(s_t1[f], 16)
            over_tiles(sp, store_table1)

            def store_out(T, u, before, f, before4):
                sp.wait_ge(s_fout, T + 1)
                if known(T, lambda t: t == NT - 1):
                    sp.dma_start(out[(NT - 1) * P:N, :], outs[0:TAIL, f, :]).then_inc(s_out[f], 16)
                else:
                    sp.dma_start(out[tile_cols(T), :], outs[:, f, :]).then_inc(s_out[f], 16)
            over_tiles(sp, store_out)
            for f in range(4):
                sp.wait_ge(s_out[f], 16 * len(range(f, NT, 4)))

        @block.gpsimd
        def _(pool):
            for k, pad in enumerate((N, 0, 0)):
                pool.memset(edge_rows[:, k, RC - 1, :], pad).then_inc(s_pads, 1)
            pool.memset(rel_sb, 0.0).then_inc(s_pads, 1)
            pool.memset(x_sb[:, NT - 1:LT, :], 0.0).then_inc(s_pads, 1)
            pool.memset(ident[:], 0.0).then_inc(s_ident, 1)
            pool.iota(iota_i, pattern=[[1, 256]], base=0, channel_multiplier=0).then_inc(s_ones, 1)
            pool.wait_ge(s_ident, 1)
            pool.affine_select(out=ident[:], in_=ident[:], compare_op=ALU.not_equal, fill=1.0, base=0,
                               pattern=[[-1, P]], channel_multiplier=1).then_inc(s_ident, 1)
            pool.memset(dst_score[:, NPAD:NACC], 0.0).then_inc(s_zero, 1)
            pool.memset(sums[:], 0.0).then_inc(s_zero, 1)
            if LT > NT:
                pool.memset(xT[:, :, NPAD:LT * P], 0.0).then_inc(s_zero, 1)
            pool.wait_ge(s_span, 1)
            pool.partition_all_reduce(span[:].rearrange("p a g -> p (a g)"),
                                      span_in[:].rearrange("p a g -> p (a g)"), P, RMAX).then_inc(s_spanned, 1)
            pool.wait_ge(s_wa, 32)
            pool.wait_ge(s_w3, 16 * (6 - KD))
            pool.tensor_tensor(w3_rest, w3_rest, a_bc.unsqueeze(1).broadcast_to([P, 6 - KD, 3 * D]),
                               ALU.mult).then_inc(s_w3a, 1)
            for h in (2, 4):
                half = 3 * D // h
                pool.wait_ge(s_w3a, h // 2)
                pool.tensor_tensor(w3_rest[:, :, 0:half], w3_rest[:, :, 0:half], w3_rest[:, :, half:2 * half],
                                   ALU.add).then_inc(s_w3a, 1)
            pool.wait_ge(s_w, 64)
            for c in range(KD):
                for w in (w_loops[:, c, c * P:(c + 1) * P], w_loops[:, c, D + c * P:D + (c + 1) * P],
                          w_l1[:, c, c * P:(c + 1) * P]):
                    last = pool.tensor_tensor(w, w, ident[:], ALU.add)
            last.then_inc(s_w_plus, 1)

            pool.wait_ge(s_passes, 1)
            n_pass = pool.value_load(passes_i[0:1, 0:1], min_val=1, max_val=MAXPASS)

            def gather(L, table, width):
                with pool.Fori(0, n_pass) as p:
                    with pool.Fori(0, ITERS) as it:
                        for s in range(SLOTS):
                            g = it * SLOTS + s
                            if L is L0 and s == 2:
                                pool.wait_ge(s_setup, 1)
                            pool.wait_ge(L.staged, p * STAGES + g + 1)
                            pool.wait_ge(L.summed, p * NG + g + 1)
                            pool.sem_inc(L.allowed, 1)
                            for k in range(GT):
                                pool.indirect_dma_start(
                                    out=rows[:, s, k, 0:width], out_offset=None, in_=table,
                                    in_offset=bass.IndirectOffsetOnAxis(ap=idx_slot[s][:, k:k + 1], axis=0),
                                ).then_inc(L.gathered[s], 16)

            for f in range(4):
                pool.wait_ge(s_t0[f], 16 * len(range(f, NT, 4)))
            gather(L0, table0, ROW0)

            def join(T, u):
                pool.wait_ge(s_parts, T + 1)
                pool.tensor_tensor(yb[:, u, 0, :], yb[:, u, 0, :], yb[:, u, 1, :], ALU.add).then_inc(s_half, 1)
                pool.wait_ge(s_half, T + 1)
                pool.tensor_tensor(yb[:, u, 3, :], yb[:, u, 0, :], yb[:, u, 2, :], ALU.add).then_inc(s_joined, 1)

            def middle(T, u, before, f, before4):
                if not known(T, lambda t: t + 2 >= NT):
                    join(T + 2, u)

            join(0, 0)
            join(1, 1)
            over_tiles(pool, middle)

            pool.wait_ge(s_acc, NT)
            pool.memset(sums[:, 0:KD, :], 0.0).then_inc(s_rezero, 1)
            for f in range(4):
                pool.wait_ge(s_t1[f], 16 * len(range(f, NT, 4)))
            gather(L1, table1, D)

        @block.scalar
        def _(act):
            def first_copy_in(T, u):
                if known(T, lambda t: t == X0):
                    act.wait_ge(s_x[3], 16)
                if known(T, lambda t: t == 2 * X0):
                    act.wait_ge(s_x[1], 16 * ((NT - 1 - 2 * X0) // 2))
                    act.wait_ge(s_x[2], 16)
                free_of(act, s_xt, T)
                nc.scalar.copy(xs[:, u, :], x_sb[:, bass.ds(T, 1), :].rearrange("p t f -> p (t f)")
                               ).then_inc(s_xs, 1)

            def first_transposed(T, u):
                act.wait_ge(s_xt, T + 1)
                free_of(act, s_tab_ps, T)
                free_of(act, s_xT, T)
                nc.scalar.copy(xTs[:, u, :, :].rearrange("p c n -> p (c n)"), ps[6 + u][:, 0:D]).then_inc(s_xTs, 1)

            def first(T, u, before, f, before4):
                if not known(T, lambda t: t + 1 >= NT):
                    first_transposed(T + 1, 1 - u)
                if known(T, lambda t: t == 2 * X0 - 2):
                    first_copy_in(2 * X0, 0)
                if not known(T, lambda t: t + 3 == 2 * X0 or t + 3 >= NT):
                    first_copy_in(T + 3, 1 - u)

            act.wait_ge(s_eps, 1)
            nc.scalar.activation(eps_t[:], ones[:, 0:1], ACT.Identity, scale=EPS)
            act.wait_ge(s_pads, 3)
            for k, e in enumerate((dst, src, etype)):
                whole = (RC - 1) * RP * P
                act.dma_start(edge_rows[:, k, 0:RC - 1, :],
                              e[0:whole].rearrange("(c r i) -> r c i", c=RC - 1, i=P)).then_inc(s_edges, 16)
                more = EFULL - (RC - 1) * RP
                act.dma_start(edge_rows[0:more, k, RC - 1, :],
                              e[whole:EFULL * P].rearrange("(r i) -> r i", i=P)).then_inc(s_edges, 16)
                act.dma_start(edge_rows[more:more + 1, k, RC - 1, 0:EREM],
                              e[EFULL * P:E].rearrange("(r i) -> r i", r=1)).then_inc(s_edges, 16)
            act.wait_ge(s_x[0], 16)
            first_copy_in(0, 0)
            first_copy_in(1, 1)
            first_transposed(0, 0)
            first_copy_in(2, 0)
            over_tiles(act, first, head=2 * X0)

            def stage(L, s, g):
                nc.scalar.copy(idx_slot[s][:], idx_tab[:, bass.ds(g * GT, GT)])
                nc.scalar.copy(tab_slot[:, s, :, :], tabs[:, :, bass.ds(g * GT, GT)]).then_inc(L.staged, 1)

            def stage_first(L, p):
                act.wait_ge(L.base, p + 1)
                for g in range(LOOK):
                    stage(L, g, g)

            act.wait_ge(s_passes, 1)
            n_pass = act.value_load(passes_i[0:1, 0:1], min_val=1, max_val=MAXPASS)
            stage_first(L0, 0)
            act.wait_ge(s_dscore, 1)
            for b in range(3):
                nc.scalar.copy(dst_score[:, b * SC:(b + 1) * SC], ps[score_bank[b]][:, :])
            act.drain()
            act.sem_inc(s_dscore_sb, 1)
            act.wait_ge(s_dscore, 2)
            for b in range(3, 5):
                nc.scalar.copy(dst_score[:, b * SC:(b + 1) * SC], ps[score_bank[b]][:, :])
            act.drain()
            act.sem_inc(s_dscore_sb, 1)

            def loop_in(T):
                nc.scalar.copy(loop_xT, xT[:, :, tile_cols(T)]).then_inc(s_loop_in, 1)

            def loop_out(T):
                act.wait_ge(s_loop_ps, T + 1)
                nc.scalar.copy(x_sb[:, bass.ds(T, 1), :].rearrange("p t f -> p (t f)"), ps[2][:, 0:D])
                nc.scalar.copy(xT[:, :, tile_cols(T)], ps[2][:, D:2 * D].rearrange("p (c n) -> p c n", c=KD))

            def edge_pass(p, messages):
                with act.Fori(0, ITERS) as it:
                    for s in range(SLOTS):
                        g = it * SLOTS + s
                        act.wait_ge(L0.score, p * NG + g + 1)
                        nc.scalar.activation(sc[:, s % 2, 2, :], sc[:, s % 2, 1, :], ACT.Exp).then_inc(L0.alpha, 1)
                        act.wait_ge(L0.summed, p * NG + g + SLOTS - 1)
                        stage(L0, (s + LOOK) % SLOTS, g + LOOK)
                        act.wait_ge(L0.staged, p * STAGES + g + 1)
                        for k in range(GT):
                            nc.scalar.activation(hot_rel[:, s % 2, k, 0:R], iota[:, 0:R], ACT.Abs,
                                                 bias=tab_slot[:, s, 2, k:k + 1])
                        act.drain()
                        nc.scalar.activation(hot_rel[:, s % 2, :, 0:R], hot_rel[:, s % 2, :, 0:R], ACT.Relu,
                                             bias=ones[:, 0:1], scale=-1.0).then_inc(L0.hot_rel, 1)
                        if messages and s % 2 == 0:
                            loop_in(it * 2 + s // 2)
                        act.wait_ge(L0.hot_dst, p * NG + g + 1)
                        nc.scalar.copy(hot_dst_b[:, s % 2, :, :], hot_dst[:, s % 2, :, :]).then_inc(L0.hot_dst_b, 1)
                        if messages and s % 2 == 1:
                            loop_out(it * 2 + s // 2)
                stage_first(L0, p + 1)

            act.wait_ge(s_dscore, 3)
            edge_pass(0, True)
            with act.If(n_pass > 1):
                with act.Fori(1, n_pass) as p:
                    edge_pass(p, False)
            act.end_ifs()

            def copy_sums(T, u):
                free_of(act, s_agg, T)
                nc.scalar.copy(acc_s[:, u, :, :], sums[:, :, tile_cols(T)]).then_inc(s_acc, 1)

            def parts(T, u):
                act.wait_ge(s_mask, T + 1)
                nc.scalar.activation(yb[:, u, 0, :], x_sb[:, bass.ds(T, 1), :].rearrange("p t f -> p (t f)"),
                                     ACT.Identity, scale=has_edges[:, u, 0:1])
                nc.scalar.activation(yb[:, u, 1, :].rearrange("p (c n) -> p c n", c=KD), xT[:, :, tile_cols(T)],
                                     ACT.Identity, scale=has_edges[:, u, 1:2])
                nc.scalar.activation(yb[:, u, 2, :], ps[0 + u][:, 0:D], ACT.Relu).then_inc(s_parts, 1)

            def deviation(T, u):
                act.wait_ge(s_var, T + 1)
                nc.scalar.activation(col[:, u, 0:1], mv[:, u, 1:2], ACT.Sqrt, bias=eps_t[:]).then_inc(s_std, 1)

            def neighbours_out(T, u, f):
                act.wait_ge(s_l1, T + 1)
                if not known(T, lambda t: t < 4):
                    act.wait_ge(s_sparse, T - 3)
                nc.scalar.copy(hn[:, f, :], ps[6 + u][:, D:2 * D]).then_inc(s_hn, 1)

            def residual_out(T, u):
                nc.scalar.copy(x_sb[:, bass.ds(T, 1), :].rearrange("p t f -> p (t f)"), ps[6 + u][:, 0:D]
                               ).then_inc(s_res, 1)

            def middle(T, u, before, f, before4):
                act.wait_ge(s_rstd, T + 1)
                nc.scalar.activation(x1s[:, u, :], yb[:, u, 3, :], ACT.Identity, bias=col[:, u, 2:3],
                                     scale=col[:, u, 1:2]).then_inc(s_x1, 1)
                act.wait_ge(s_x1t, T + 1)
                free_of(act, s_l1, T)
                nc.scalar.copy(x1Ts[:, u, :], ps[4 + u][:, 0:D]).then_inc(s_x1T, 1)
                if not known(T, lambda t: t + 2 >= NT):
                    parts(T + 2, u)
                if not known(T, lambda t: t + 1 >= NT):
                    deviation(T + 1, 1 - u)
                if not known(T, lambda t: t == 0):
                    neighbours_out(T - 1, 1 - u, (f - 1) % 4)
                    residual_out(T - 1, 1 - u)
                if not known(T, lambda t: t + 4 >= NT):
                    copy_sums(T + 4, u)

            nc.scalar.activation(root[:], ones[:, 0:1], ACT.Sqrt)
            act.wait_ge(L0.added, n_pass * (NG + 1) + 1)
            for T in range(2):
                copy_sums(T, T)
            for T in range(2):
                parts(T, T)
                copy_sums(T + 2, T)
            deviation(0, 0)
            stage_first(L1, 0)
            over_tiles(act, middle, head=5)
            neighbours_out(NT - 1, (NT - 1) % 2, (NT - 1) % 4)
            residual_out(NT - 1, (NT - 1) % 2)

            with act.Fori(0, n_pass) as p:
                with act.Fori(0, ITERS) as it:
                    for s in range(SLOTS):
                        g = it * SLOTS + s
                        act.wait_ge(L1.summed, p * NG + g + SLOTS - 1)
                        stage(L1, (s + LOOK) % SLOTS, g + LOOK)
                stage_first(L1, p + 1)

            def copy_last(T, f):
                if not known(T, lambda t: t < 4):
                    act.wait_ge(s_fagg, T - 3)
                nc.scalar.copy(acc_last[:, f, :, :], sums[:, 0:KD, tile_cols(T)]).then_inc(s_facc, 1)

            def write_out(T, u, f, before4):
                act.wait_ge(s_frstd, T + 1)
                if not known(T, lambda t: t < 4):
                    act.wait_ge(s_out[f], 16 * before4)
                nc.scalar.activation(outs[:, f, :], last_rows_sb[:, f, :], ACT.Identity, bias=col[:, u, 2:3],
                                     scale=col[:, u, 1:2]).then_inc(s_fout, 1)

            def last(T, u, before, f, before4):
                if not known(T, lambda t: t + 3 >= NT):
                    copy_last(T + 3, (f + 3) % 4)
                act.wait_ge(s_fvar, T + 1)
                nc.scalar.activation(col[:, u, 0:1], mv[:, u, 1:2], ACT.Sqrt, bias=eps_t[:]).then_inc(s_fstd, 1)
                if not known(T, lambda t: t == 0):
                    write_out(T - 1, 1 - u, (f - 1) % 4, before4 - (f == 0))

            act.wait_ge(L1.added, n_pass * (NG + 1) + 1)
            for T in range(3):
                copy_last(T, T)
            over_tiles(act, last)
            write_out(NT - 1, (NT - 1) % 2, (NT - 1) % 4, (NT - 1) // 4)

        @block.tensor
        def _(pe):
            pe.sem_inc(L0.summed, SLOTS)
            pe.sem_inc(L1.summed, SLOTS)

            def transpose_edges():
                pe.wait_ge(s_edge_f, 1)
                for k in range(3):
                    for c in range(RC):
                        last = nc.tensor.transpose(ps[3 + k][:, c * RP:(c + 1) * RP], edge_f[:, k, c, :],
                                                   ident[0:RP, 0:RP])
                last.then_inc(s_edge_t, 1)

            def transpose_x(T, u):
                pe.wait_ge(s_xs, T + 1)
                free_of(pe, s_xTs, T)
                for c in range(KD):
                    last = nc.tensor.transpose(ps[6 + u][:, c * P:(c + 1) * P], xs[:, u, c * P:(c + 1) * P], ident[:])
                last.then_inc(s_xt, 1)

            def first(T, u, before, f, before4):
                early = not known(T, lambda t: 2 * X0 - 2 <= t < 2 * X0)
                if early and not known(T, lambda t: t + 2 >= NT):
                    transpose_x(T + 2, u)
                pe.wait_ge(s_xTs, T + 1)
                free_of(pe, s_tab_sb, T)
                for c in range(KD):
                    last = nc.tensor.matmul(ps[0 + u][:, 0:D + 1], xTs[:, u, c, :], w_tab[:, c, :],
                                            start=(c == 0), stop=(c == KD - 1))
                last.then_inc(s_tab_ps, 1)
                if known(T, lambda t: t == 5):
                    transpose_edges()
                if not early:
                    transpose_x(T + 2, u)

            pe.wait_ge(s_ident, 2)
            transpose_x(0, 0)
            transpose_x(1, 1)
            pe.wait_ge(s_wn, 16)
            pe.wait_ge(s_wsrc, 1)
            over_tiles(pe, first, head=2 * X0)

            pe.wait_ge(s_xT, NT)
            pe.wait_ge(s_rel, 32)
            for r in range(2):
                for c in range(KD):
                    last = nc.tensor.transpose(ps[7][:, (2 * c + r) * P:(2 * c + r + 1) * P],
                                               rel_sb[:, r, c * P:(c + 1) * P], ident[:])
            last.then_inc(s_relT, 1)
            pe.wait_ge(s_wvec, 1)
            pe.wait_ge(s_tab_sb, NT)
            pe.wait_ge(s_span, 1)

            def dst_scores(blocks):
                for b in blocks:
                    n = min(NPAD, (b + 1) * SC) - b * SC
                    for c in range(KD):
                        last = nc.tensor.matmul(ps[score_bank[b]][:, 0:n], wd_bc[:, c, :],
                                                xT[:, c, b * SC:b * SC + n], start=(c == 0), stop=(c == KD - 1))
                last.then_inc(s_dscore, 1)

            dst_scores(range(3))
            pe.wait_ge(s_relT_sb, 1)
            for c in range(KD):
                nc.tensor.matmul(ps[7][:, 0:R], wr_bc[:, c, :], relT[:, c, 0:R],
                                 start=(c == 0), stop=(c == KD - 1))
            for r in range(2):
                for c in range(KD):
                    last = nc.tensor.matmul(ps[3][:, r * D:(r + 1) * D], relT[:, c, r * P:(r + 1) * P],
                                            w_tab[:, c, 0:D], start=(c == 0), stop=(c == KD - 1))
            last.then_inc(s_relp, 1)
            dst_scores(range(3, 5))
            pe.wait_ge(s_dscore_sb, 1)
            dst_scores(range(5, 7))

            pe.wait_ge(s_setup, 2)
            pe.wait_ge(s_passes, 1)
            n_pass = pe.value_load(passes_i[0:1, 0:1], min_val=1, max_val=MAXPASS)
            def loop_messages(T):
                pe.wait_ge(s_loop_in, T + 1)
                for c in range(KD):
                    last = nc.tensor.matmul(ps[2][:, :], loop_xT[:, c, :], w_loops[:, c, :],
                                            start=(c == 0), stop=(c == KD - 1))
                last.then_inc(s_loop_ps, 1)

            def edge_pass(p, messages):
                with pe.Fori(0, ITERS) as it:
                    for s in range(SLOTS):
                        g = it * SLOTS + s
                        if messages and s % 2 == 1:
                            loop_messages(it * 2 + s // 2)
                        pe.wait_ge(L0.added, p * (NG + 1) + g + 1)
                        pe.wait_ge(L0.hot_dst, p * NG + g + 1)
                        for q in range(KD):
                            for k in range(GT):
                                nc.tensor.matmul(ps[s % 2][:, q * P:(q + 1) * P], rows[:, s, k, q * P:(q + 1) * P],
                                                 hot_dst[:, s % 2, k, :], start=(k == 0), stop=(k == GT - 1))
                        pe.wait_ge(L0.hot_rel, p * NG + g + 1)
                        pe.wait_ge(L0.hot_dst_b, p * NG + g + 1)
                        for r in range(2):
                            for k in range(GT):
                                last = nc.tensor.matmul(ps[s % 2][:, (KD + r) * P:(KD + r + 1) * P],
                                                        hot_rel[:, s % 2, k, r * P:(r + 1) * P],
                                                        hot_dst_b[:, s % 2, k, :], start=(k == 0), stop=(k == GT - 1))
                        last.then_inc(L0.summed, 1)

            pe.wait_ge(s_w_plus, 1)
            edge_pass(0, True)
            with pe.If(n_pass > 1):
                with pe.Fori(1, n_pass) as p:
                    edge_pass(p, False)
            pe.end_ifs()

            def node_products(T, u):
                pe.wait_ge(s_acc, T + 1)
                if not known(T, lambda t: t < 2):
                    pe.wait_ge(s_parts, T - 1)
                for r in range(2):
                    nc.tensor.matmul(ps[0 + u][:, 0:D + 1], acc_s[:, u, KD + r, :], rel_tab[:, r, :],
                                     start=(r == 0), stop=False)
                for c in range(KD):
                    last = nc.tensor.matmul(ps[0 + u][:, c * P:(c + 1) * P], acc_s[:, u, c, :], ident[:],
                                            start=False, stop=(c == KD - 1))
                last.then_inc(s_agg, 1)

            def middle(T, u, before, f, before4):
                pe.wait_ge(s_x1, T + 1)
                free_of(pe, s_x1T, T)
                for c in range(KD):
                    last = nc.tensor.transpose(ps[4 + u][:, c * P:(c + 1) * P], x1s[:, u, c * P:(c + 1) * P], ident[:])
                last.then_inc(s_x1t, 1)
                if not known(T, lambda t: t + 3 >= NT):
                    node_products(T + 3, 1 - u)
                pe.wait_ge(s_x1T, T + 1)
                free_of(pe, s_res, T)
                for c in range(KD):
                    last = nc.tensor.matmul(ps[6 + u][:, :], x1Ts[:, u, c * P:(c + 1) * P], w_l1[:, c, :],
                                            start=(c == 0), stop=(c == KD - 1))
                last.then_inc(s_l1, 1)

            node_products(0, 0)
            node_products(1, 1)
            node_products(2, 0)
            over_tiles(pe, middle)

            pe.wait_ge(s_parts, NT)
            with pe.Fori(0, n_pass) as p:
                with pe.Fori(0, ITERS) as it:
                    for s in range(SLOTS):
                        g = it * SLOTS + s
                        pe.wait_ge(L1.added, p * (NG + 1) + g + 1)
                        pe.wait_ge(L1.hot_dst, p * NG + g + 1)
                        pe.wait_ge(L1.gathered[s], (p * ITERS + it + 1) * GT * 16)
                        for q in range(KD):
                            for k in range(GT):
                                last = nc.tensor.matmul(ps[s % 2][:, q * P:(q + 1) * P],
                                                        rows[:, s, k, q * P:(q + 1) * P], hot_dst[:, s % 2, k, :],
                                                        start=(k == 0), stop=(k == GT - 1))
                        last.then_inc(L1.summed, 1)

            def last_rows(T, u, before, f, before4):
                pe.wait_ge(s_facc, T + 1)
                if not known(T, lambda t: t < 3):
                    pe.wait_ge(s_fvar, T - 2)
                for c in range(KD):
                    last = nc.tensor.transpose(ps[4 + f][:, c * P:(c + 1) * P], acc_last[:, f, c, :], ident[:])
                last.then_inc(s_fagg, 1)
            over_tiles(pe, last_rows)

        @block.vector
        def _(dve):
            V = nc.vector

            def settle():
                dve.drain()

            V.memset(ones[:], 1.0).then_inc(s_eps, 1)
            V.memset(tab_out[:], 0.0)

            dve.wait_ge(s_wa, 32)
            for c in range(KD):
                V.tensor_tensor_reduce(out=w3_first[:, c, :], in0=w3_first[:, c, :], in1=a_bc, scale=1.0, scalar=0.0,
                                       op0=ALU.mult, op1=ALU.add, accum_out=w_vec[:, c:c + 1])
            settle()
            V.tensor_copy(w_tab[:, :, D:D + 1].rearrange("p c o -> p (c o)"), w_vec[:, 0:KD]).then_inc(s_wsrc, 1)
            V.memset(tabs[:], 0.0)
            V.memset(idx_tab[:], 0)
            V.memset(base_i[:], 0)
            dve.wait_ge(s_ones, 1)
            V.tensor_copy(iota[:], iota_i)

            def edge_floats():
                dve.wait_ge(s_edges, 9 * 16)
                V.tensor_copy(edge_f[:, :, :, :].rearrange("r k c i -> r k (c i)"),
                              edge_rows[:, :, :, :].rearrange("r k c i -> r k (c i)")).then_inc(s_edge_f, 1)

            def edge_tables():
                dve.wait_ge(s_edge_t, 1)
                V.tensor_copy(dst_f[:], ps[3][:, 0:NE])
                V.tensor_copy(idx_tab[:, 0:NE], ps[4][:, 0:NE])
                V.tensor_copy(tabs[:, 1, 0:NE], ps[5][:, 0:NE])

            def edge_spans():
                settle()
                V.tensor_scalar(tabs[:, 2, 0:NE], tabs[:, 1, 0:NE], -1.0, None, ALU.mult)
                V.memset(hot_rel[:, :, :, R:256], 0.0)
                V.tensor_reduce(span_in[:, 1, :], dst_f[:].rearrange("p (g k) -> p g k", k=GT), AX.X, ALU.max)
                V.tensor_reduce(base_cur[:], dst_f[:].rearrange("p (g k) -> p g k", k=GT), AX.X, ALU.min)
                settle()
                V.tensor_scalar(span_in[:, 0, :], base_cur[:], -1.0, None, ALU.mult).then_inc(s_span, 1)

            def count_passes():
                dve.wait_ge(s_spanned, 1)
                V.tensor_tensor(base_cur[:], span[:, 0, :], span[:, 1, :], ALU.add)
                settle()
                V.reduce_max(flags[:, 0:1], base_cur[:], AX.X)
                settle()
                V.tensor_scalar(flags[:, 1:2], flags[:, 0:1], float(P), None, ALU.is_ge)
                V.tensor_scalar(flags[:, 2:3], flags[:, 0:1], float(P), None, ALU.is_lt)
                settle()
                V.tensor_scalar(passes_i[:], flags[:, 1:2], float(MAXPASS - 1), 1.0, ALU.mult, ALU.add)
                V.tensor_scalar(base0[:], span[:, 0, :], flags[:, 2:3], -1.0, ALU.mult, ALU.mult)
                settle()
                V.sem_inc(s_passes, 1)

            def set_windows(L):
                V.tensor_copy(base_i[:, 1:1 + NG], base_cur[:])
                V.tensor_tensor(tabs[:, 0, 0:NE].rearrange("p (g k) -> p g k", k=GT),
                                dst_f[:].rearrange("p (g k) -> p g k", k=GT),
                                base_cur[:].unsqueeze(2).broadcast_to([P, NG, GT]), ALU.subtract)
                settle()
                dve.sem_inc(L.base, 1)

            def begin_layer(L):
                V.tensor_copy(base_cur[:], base0[:])
                settle()
                set_windows(L)

            def first(T, u, before, f, before4):
                dve.wait_ge(s_xTs, T + 1)
                V.tensor_copy(xT[:, :, tile_cols(T)], xTs[:, u, :, :]).then_inc(s_xT, 1)
                dve.wait_ge(s_tab_ps, T + 1)
                if not known(T, lambda t: t < 4):
                    dve.wait_ge(s_t0[f], before4 * 16)
                V.tensor_copy(tab_out[:, f, 0:D + 1], ps[0 + u][:, 0:D + 1]).then_inc(s_tab_sb, 1)
                if known(T, lambda t: t == 4):
                    edge_floats()
                if known(T, lambda t: t == 6):
                    edge_tables()
                if known(T, lambda t: t == 7):
                    edge_spans()
                if known(T, lambda t: t == NT - 5):
                    count_passes()
                    begin_layer(L0)
            over_tiles(dve, first, head=2 * X0)

            dve.wait_ge(s_w3a, 3)
            V.tensor_reduce(w_vec[:, KD:6], w3_rest[:, :, 0:3 * D // 4], AX.X, ALU.add)
            settle()
            for c in range(KD):
                V.tensor_scalar(wd_bc[:, c, :], ones[:], w_vec[:, 2 + c:3 + c], None, ALU.mult)
                last = V.tensor_scalar(wr_bc[:, c, :], ones[:], w_vec[:, 4 + c:5 + c], None, ALU.mult)
            last.then_inc(s_wvec, 1)
            dve.wait_ge(s_relT, 1)
            V.tensor_copy(relT.rearrange("p c r -> p (c r)"), ps[7][:, :]).then_inc(s_relT_sb, 1)
            dve.wait_ge(s_relp, 1)
            V.tensor_copy(rel_score[:], ps[7][:, 0:R])
            V.memset(rel_tab[:, :, D:D + 1], 1.0)
            V.tensor_copy(rel_tab[:, :, 0:D], ps[3][:, :].rearrange("p (r f) -> p r f", r=2)).then_inc(s_setup, 1)
            dve.wait_ge(s_dscore, 3)
            for b in range(5, 7):
                n = min(NPAD, (b + 1) * SC) - b * SC
                last = V.tensor_copy(dst_score[:, b * SC:b * SC + n], ps[score_bank[b]][:, 0:n])
            last.then_inc(s_setup, 1)
            dve.wait_ge(s_dscore_sb, 2)
            for f in range(4):
                dve.wait_ge(s_t0[f], 16 * len(range(f, NT, 4)))

            dve.wait_ge(s_zero, 2)
            dve.sem_inc(L0.added, 1)
            dve.sem_inc(L1.added, 1)
            n_pass = dve.value_load(passes_i[0:1, 0:1], min_val=1, max_val=MAXPASS)

            def window_before(g):
                return dve.value_load(base_i[0:1, bass.ds(g, 1)], min_val=0, max_val=N)

            def add_window(L, p, g, s, width, base):
                dve.wait_ge(L.added, p * (NG + 1) + g + 1)
                dve.wait_ge(L.summed, p * NG + g + SLOTS)
                win = sums[:, 0:width, bass.ds(base, P)]
                V.tensor_tensor(win, win, ps[(s + 1) % 2][:, 0:width * P].rearrange("p (q n) -> p q n", n=P),
                                ALU.add).then_inc(L.added, 1)

            def end_pass(L, p):
                dve.wait_ge(L.staged, (p + 1) * STAGES)
                V.tensor_scalar(base_cur[:], base_cur[:], float(P), None, ALU.add)
                settle()
                set_windows(L)

            def window_base(g):
                return dve.value_load(base_i[0:1, bass.ds(g + 1, 1)], min_val=0, max_val=N)

            def look_up(base, b, s, k, which):
                if which == "dst":
                    return V.scalar_tensor_tensor(out=products_d[:, k, :], in0=iota[:, 0:P],
                                                  scalar=tab_slot[:, s, 0, k:k + 1],
                                                  in1=dst_score[:, bass.ds(base, P)], op0=ALU.is_equal,
                                                  op1=ALU.mult, accum_out=score_dst[:, b, k:k + 1])
                return V.scalar_tensor_tensor(out=products_r[:, k, :], in0=iota[:, 0:R],
                                              scalar=tab_slot[:, s, 1, k:k + 1], in1=rel_score[:],
                                              op0=ALU.is_equal, op1=ALU.mult, accum_out=score_rel[:, b, k:k + 1])

            with dve.Fori(0, n_pass) as p:
                dve.wait_ge(L0.added, p * (NG + 1) + 1)
                V.memset(ps[1][:, :], 0.0)
                settle()
                base = window_base(0)
                dve.wait_ge(L0.staged, p * STAGES + 1)
                for which in ("dst", "rel"):
                    for k in range(GT):
                        last = look_up(base, 0, 0, k, which)
                last.then_inc(L0.looked_up, 1)
                with dve.Fori(0, ITERS) as it:
                    for s in range(SLOTS):
                        g = it * SLOTS + s
                        b, b1, s1 = s % 2, (s + 1) % 2, (s + 1) % SLOTS
                        base = window_base(g + 1)
                        nth = dve.snap(p * NG + g + 1)
                        looked = dve.snap(p * (NG + 1) + g + 1)
                        dve.wait_ge(L0.staged, p * STAGES + g + 2)
                        dve.wait_ge(L0.looked_up, looked)
                        look_up(base, b1, s1, 0, "dst")
                        V.tensor_tensor(sc[:, b, 0, :], score_dst[:, b, :], score_rel[:, b, :],
                                        ALU.add).then_inc(L0.joined, 1)
                        look_up(base, b1, s1, 1, "dst")
                        dve.wait_ge(L0.gathered[s], (p * ITERS + it + 1) * GT * 16)
                        dve.wait_ge(L0.joined, nth)
                        V.tensor_tensor(sc[:, b, 0, :], sc[:, b, 0, :], rows[:, s, :, D], ALU.add).then_inc(L0.scored, 1)
                        look_up(base, b1, s1, 2, "dst")
                        dve.wait_ge(L0.scored, nth)
                        V.scalar_tensor_tensor(out=sc[:, b, 1, :], in0=sc[:, b, 0, :], scalar=0.01,
                                               in1=sc[:, b, 0, :], op0=ALU.mult, op1=ALU.max).then_inc(L0.score, 1)
                        for k in (3, 4):
                            look_up(base, b1, s1, k, "dst")
                        dve.wait_ge(L0.alpha, nth)
                        V.tensor_scalar(sc[:, b, 3, :], sc[:, b, 2, :], 0.25, None, ALU.mult).then_inc(L0.quarter, 1)
                        look_up(base, b1, s1, 5, "dst")
                        dve.wait_ge(L0.quarter, nth)
                        V.reciprocal(sc[:, b, 4, :], sc[:, b, 3, :]).then_inc(L0.inverse, 1)
                        look_up(base, b1, s1, 6, "dst")
                        dve.wait_ge(L0.inverse, nth)
                        V.tensor_tensor(sc[:, b, 5, :], sc[:, b, 3, :], sc[:, b, 4, :], ALU.mult).then_inc(L0.weight, 1)
                        look_up(base, b1, s1, 7, "dst")
                        dve.wait_ge(L0.summed, p * NG + g + SLOTS - 1)
                        dve.wait_ge(L0.weight, nth)
                        for k in range(GT):
                            last = V.tensor_scalar(hot_dst[:, b, k, :], iota[:, 0:P], tab_slot[:, s, 0, k:k + 1],
                                                   sc[:, b, 5, k:k + 1], ALU.is_equal, ALU.mult)
                        last.then_inc(L0.hot_dst, 1)
                        for k in range(GT):
                            last = look_up(base, b1, s1, k, "rel")
                        last.then_inc(L0.looked_up, 1)
                        add_window(L0, p, g, s, 4, window_before(g))
                last_base = window_before(NG)
                end_pass(L0, p)
                add_window(L0, p, NG, NG, 4, last_base)

            def write_sparse(T, f, before4=None):
                if known(T, lambda t: t >= 4):
                    dve.wait_ge(s_t1[f], T // 4 * 16)
                elif not isinstance(T, int):
                    dve.wait_ge(s_t1[(f - 1) % 4], before4 * 16)
                V.scalar_tensor_tensor(out=sparse[:, f, :], in0=work[:, f, :], scalar=LOWEST, in1=hn[:, f, :],
                                       op0=ALU.is_equal, op1=ALU.mult).then_inc(s_sparse, 1)

            def counts(T, u):
                dve.wait_ge(s_agg, T + 1)
                V.tensor_scalar(has_edges[:, u, 0:1], ps[0 + u][:, D:D + 1], 0.0, None, ALU.is_gt)
                V.tensor_scalar(has_edges[:, u, 1:2], ps[0 + u][:, D:D + 1], 0.0, None, ALU.is_le)
                V.tensor_scalar(degree[:, bass.ds(T, 1)], ps[0 + u][:, D:D + 1], 1.0, None,
                                ALU.max).then_inc(s_mask, 1)

            def statistics(T, u):
                dve.wait_ge(s_joined, T + 1)
                V.bn_stats(bn[:, u, :], yb[:, u, 3, :])

            def inverse_std(T, u):
                dve.wait_ge(s_std, T + 1)
                V.reciprocal(col[:, u, 1:2], col[:, u, 0:1])

            def mean_over_std(T, u):
                V.tensor_scalar(col[:, u, 2:3], mv[:, u, 0:1], col[:, u, 1:2], -1.0, ALU.mult,
                                ALU.mult).then_inc(s_rstd, 1)

            def middle(T, u, before, f, before4):
                v = 1 - u
                stats = not known(T, lambda t: t + 1 >= NT)
                rounds = [r for r in reversed(range(TOPK // 8)) if not known(T, lambda t: not 0 <= t - 1 - r < NT)]

                def slot_source(r):
                    slot = (f - 1 - r) % 4
                    return slot, hn[:, slot, :] if r == 0 else work[:, slot, :]

                def find(r):
                    slot, source = slot_source(r)
                    V.max(top8[:, slot, :], source)

                if stats:
                    statistics(T + 1, v)
                settle()
                if not known(T, lambda t: t < 5):
                    write_sparse(T - 5, (f - 5) % 4, before4 - (f < 2))
                if stats:
                    V.bn_aggr(mv[:, v, :], bn[:, v, :]).then_inc(s_var, 1)
                for r in rounds:
                    if r > 0:
                        find(r)
                if 0 in rounds:
                    dve.wait_ge(s_hn, T)
                if stats:
                    inverse_std(T + 1, v)
                if 0 in rounds:
                    find(0)
                settle()
                if stats:
                    mean_over_std(T + 1, v)
                for r in rounds:
                    slot, source = slot_source(r)
                    V.match_replace(work[:, slot, :], top8[:, slot, :], source, LOWEST)
                if not known(T, lambda t: t + 3 >= NT):
                    counts(T + 3, v)

            dve.wait_ge(L0.staged, n_pass * STAGES + LOOK)
            begin_layer(L1)
            counts(0, 0)
            counts(1, 1)
            statistics(0, 0)
            settle()
            V.bn_aggr(mv[:, 0, :], bn[:, 0, :]).then_inc(s_var, 1)
            inverse_std(0, 0)
            settle()
            mean_over_std(0, 0)
            counts(2, 0)
            over_tiles(dve, middle, head=6)
            for T in range(NT, NT + 4):
                middle(T, T % 2, T // 2, T % 4, T // 4)
            settle()
            write_sparse(NT - 1, (NT - 1) % 4)
            V.reciprocal(r_deg[:], degree[:])

            dve.wait_ge(s_rezero, 1)
            with dve.Fori(0, n_pass) as p:
                dve.wait_ge(L1.added, p * (NG + 1) + 1)
                V.memset(ps[1][:, :], 0.0)
                settle()
                with dve.Fori(0, ITERS) as it:
                    for s in range(SLOTS):
                        g = it * SLOTS + s
                        dve.wait_ge(L1.staged, p * STAGES + g + 1)
                        dve.wait_ge(L1.summed, p * NG + g + SLOTS - 1)
                        V.tensor_tensor(hot_dst[:, s % 2, :, :], iota[:, 0:P].unsqueeze(1).broadcast_to([P, GT, P]),
                                        tab_slot[:, s, 0, :].unsqueeze(2).broadcast_to([P, GT, P]),
                                        ALU.is_equal).then_inc(L1.hot_dst, 1)
                        add_window(L1, p, g, s, KD, window_before(g))
                last_base = window_before(NG)
                end_pass(L1, p)
                add_window(L1, p, NG, NG, KD, last_base)

            def scale_of(T, u):
                V.tensor_scalar(col[:, u, 2:3], mv[:, u, 0:1], col[:, u, 1:2], -1.0, ALU.mult,
                                ALU.mult).then_inc(s_frstd, 1)

            def add_mean(T, f):
                dve.wait_ge(s_fagg, T + 1)
                if not known(T, lambda t: t < 4):
                    dve.wait_ge(s_fout, T - 3)
                V.scalar_tensor_tensor(out=last_rows_sb[:, f, :], in0=ps[4 + f][:, 0:D], scalar=r_deg[:, bass.ds(T, 1)],
                                       in1=x_sb[:, bass.ds(T, 1), :].rearrange("p t f -> p (t f)"),
                                       op0=ALU.mult, op1=ALU.add)

            def last(T, u, before, f, before4):
                V.bn_stats(bn[:, u, :], last_rows_sb[:, f, :])
                if not known(T, lambda t: t + 1 >= NT):
                    add_mean(T + 1, (f + 1) % 4)
                if not known(T, lambda t: t == 0):
                    dve.wait_ge(s_fstd, T)
                    V.reciprocal(col[:, 1 - u, 1:2], col[:, 1 - u, 0:1])
                settle()
                V.bn_aggr(mv[:, u, :], bn[:, u, :]).then_inc(s_fvar, 1)
                if not known(T, lambda t: t == 0):
                    scale_of(T - 1, 1 - u)

            add_mean(0, 0)
            settle()
            over_tiles(dve, last)
            dve.wait_ge(s_fstd, NT)
            V.reciprocal(col[:, (NT - 1) % 2, 1:2], col[:, (NT - 1) % 2, 0:1])
            settle()
            scale_of(NT - 1, (NT - 1) % 2)


_INS = ["x", "src", "dst", "edge_type_200", "L0_gnn_rel_emb", "L0_gnn_weight_neighbor", "L0_gnn_a", "L0_gnn_W3",
        "L0_gnn_loop_weight", "L0_gnn_evolve_loop_weight", "L1_gnn_W_self", "L1_gnn_W_neigh"]


def kernel(**inputs):
    import numpy as _np
    import concourse.bacc as _bacc
    from concourse import mybir as _mybir
    from concourse.bass_utils import run_bass_kernel_spmd as _run

    nc = _bacc.Bacc("TRN2", target_bir_lowering=False, num_devices=1)
    arrays, args = {}, []
    for name in _INS:
        arr = _np.ascontiguousarray(inputs[name])
        arrays[f"in_{name}_dram"] = arr
        args.append(nc.dram_tensor(f"in_{name}_dram", arr.shape, _mybir.dt.from_np(arr.dtype),
                                   kind="ExternalInput").ap())
    args.append(nc.dram_tensor("out_0_dram", tuple(inputs["x"].shape), _mybir.dt.float32,
                               kind="ExternalOutput").ap())
    gnn_two_layers(nc, *args)
    r = _run(nc, [arrays], core_ids=[0])
    return r.results[0]["out_0_dram"]
```
